# Optimizing a Trainium2 kernel written in Bass

```python
import numpy as np
import jax
import jax.numpy as jnp

def _softmax(x, axis=-1):
    return jax.nn.softmax(x, axis=axis)

def _gelu(x):
    return jax.nn.gelu(x, approximate=True)

def _silu(x):
    return jax.nn.silu(x)

def _sigmoid(x):
    return jax.nn.sigmoid(x)

def _layernorm(x, axis=-1, eps=1e-05):
    m = jnp.mean(x, axis=axis, keepdims=True)
    v = jnp.var(x, axis=axis, keepdims=True)
    return (x - m) / jnp.sqrt(v + eps)

def _scatter_add(tgt, idx, src, axis=0):
    return tgt.at[idx].add(src)

def _segment_sum(src, seg, n):
    return jax.ops.segment_sum(src, seg, n)
kernel_name = 'mk_xattn_ffn_d2_seqx_r8_f94c9b'

def setup_inputs(seed: int=0):
    np.random.seed(seed)
    _w = jnp.asarray

    def _rec_inputs():
        import jax
        import jax.numpy as jnp
        _rk = jax.random.key(seed)
        x = -0.0002928 + 1 * jax.random.normal(jax.random.fold_in(_rk, 1), (128, 64, 128), jnp.float32)
        _lenS = 64 - jax.random.randint(jax.random.fold_in(_rk, 7), (128,), 0, max(1, 64 // 4) + 1, jnp.int32)
        _lenS2 = 64 - jax.random.randint(jax.random.fold_in(_rk, 8), (128,), 0, max(1, 64 // 4) + 1, jnp.int32)
        _ctx_1024P = jax.random.normal(jax.random.fold_in(_rk, 11), (128, 16, 128), jnp.float32)
        _ctx_1024c = jax.random.dirichlet(jax.random.fold_in(_rk, 511), 0.3 * jnp.ones((16,), jnp.float32), (128, 64))
        _ctx_1024t = jnp.einsum('bsk,bkd->bsd', _ctx_1024c, _ctx_1024P)
        _ctx_1024t = _ctx_1024t * jax.lax.rsqrt(jnp.mean(jnp.square(_ctx_1024t)) + 1e-12) * 0.953939
        ctx_1024 = -1.52775e-05 + 0.999936 * (_ctx_1024t + 0.3 * jax.random.normal(jax.random.fold_in(_rk, 611), (128, 64, 128), jnp.float32))
        return (x, ctx_1024)
    x, ctx_1024 = _rec_inputs()

    def _L0_xattn_setup():
        import jax, jax.numpy as jnp
        import numpy as np
        DIM = 128
        NUM_HEADS = 8
        HEAD_DIM = 64
        INNER = NUM_HEADS * HEAD_DIM
        key = jax.random.key(seed)
        ks = jax.random.split(key, 7)
        B, N, M = (8, 64, 512)
        x = jax.random.normal(ks[0], (B, N, DIM), dtype=jnp.float32)
        context = jax.random.normal(ks[1], (B, M, DIM), dtype=jnp.float32)
        s_in = 1.0 / np.sqrt(DIM)
        s_inner = 1.0 / np.sqrt(INNER)
        Wq = jax.random.normal(ks[2], (DIM, INNER), dtype=jnp.float32) * s_in
        Wk = jax.random.normal(ks[3], (DIM, INNER), dtype=jnp.float32) * s_in
        Wv = jax.random.normal(ks[4], (DIM, INNER), dtype=jnp.float32) * s_in
        Wo = jax.random.normal(ks[5], (INNER, DIM), dtype=jnp.float32) * s_inner
        bo = jax.random.normal(ks[6], (DIM,), dtype=jnp.float32) * 0.01
        return {'x': x, 'context': context, 'Wq': Wq, 'Wk': Wk, 'Wv': Wv, 'Wo': Wo, 'bo': bo}
    _L0_xattn_all = _L0_xattn_setup()
    _L0_xattn_in = {k: v for k, v in _L0_xattn_all.items() if k in ('Wq', 'Wk', 'Wv', 'Wo', 'bo')}
    del _L0_xattn_all

    def _L0_ffn_setup():
        import jax, jax.numpy as jnp
        import numpy as np
        ALPHA = 1.702
        LIMIT = 7.0
        EPS = 1e-05
        E = 16
        K = 4

        def _swiglu(h):
            x_glu = jnp.minimum(h[..., ::2], LIMIT)
            x_lin = jnp.clip(h[..., 1::2], LIMIT, LIMIT)
            return x_glu * jax.nn.sigmoid(ALPHA * x_glu) * (x_lin + 1.0)
        key = jax.random.key(seed)
        ks = jax.random.split(key, 7)
        B, T, H, I = (1, 256, 128, 128)
        x = jax.random.normal(ks[0], (B, T, H), jnp.float32)
        scale = jnp.ones((H,), jnp.float32)
        gate_w = jax.random.normal(ks[1], (E, H), jnp.float32) * 0.02
        gate_b = jnp.zeros((E,), jnp.float32)
        mlp1_w = jax.random.normal(ks[2], (E, 2 * I, H), jnp.float32) * 0.02
        mlp1_b = jax.random.normal(ks[3], (E, 2 * I), jnp.float32) * 0.02
        mlp2_w = jax.random.normal(ks[4], (E, H, I), jnp.float32) * 0.02
        mlp2_b = jax.random.normal(ks[5], (E, H), jnp.float32) * 0.02
        return dict(x=x, scale=scale, gate_w=gate_w, gate_b=gate_b, mlp1_w=mlp1_w, mlp1_b=mlp1_b, mlp2_w=mlp2_w, mlp2_b=mlp2_b)
    _L0_ffn_all = _L0_ffn_setup()
    _L0_ffn_in = {k: v for k, v in _L0_ffn_all.items() if k in ('scale', 'gate_w', 'gate_b', 'mlp1_w', 'mlp1_b', 'mlp2_w', 'mlp2_b')}
    del _L0_ffn_all

    def _L1_xattn_setup():
        import jax, jax.numpy as jnp
        import numpy as np
        D_MODEL = 128
        NUM_HEADS = 16
        HEAD_DIM = D_MODEL // NUM_HEADS
        key = jax.random.key(seed)
        ks = jax.random.split(key, 8)
        B, S = (2, 256)
        scale = 1.0 / np.sqrt(D_MODEL)
        return {'query': jax.random.normal(ks[0], (B, S, D_MODEL), dtype=jnp.float32), 'key': jax.random.normal(ks[1], (B, S, D_MODEL), dtype=jnp.float32), 'value': jax.random.normal(ks[2], (B, S, D_MODEL), dtype=jnp.float32), 'Wq': jax.random.normal(ks[3], (D_MODEL, D_MODEL), dtype=jnp.float32) * scale, 'Wk': jax.random.normal(ks[4], (D_MODEL, D_MODEL), dtype=jnp.float32) * scale, 'Wv': jax.random.normal(ks[5], (D_MODEL, D_MODEL), dtype=jnp.float32) * scale, 'Wo': jax.random.normal(ks[6], (D_MODEL, D_MODEL), dtype=jnp.float32) * scale, 'bo': jax.random.normal(ks[7], (D_MODEL,), dtype=jnp.float32) * scale}
    _L1_xattn_all = _L1_xattn_setup()
    _L1_xattn_in = {k: v for k, v in _L1_xattn_all.items() if k in ('Wq', 'Wk', 'Wv', 'Wo', 'bo')}
    del _L1_xattn_all

    def _L1_ffn_setup():
        import jax, jax.numpy as jnp
        import numpy as np
        TOP_K = 2
        key = jax.random.key(seed)
        k1, k2, k3, k4 = jax.random.split(key, 4)
        B, S, D, F, E = (2, 256, 128, 512, 8)
        x = jax.random.normal(k1, (B, S, D), dtype=jnp.float32)
        choice = jax.random.normal(k2, (E, D), dtype=jnp.float32) / np.sqrt(D)
        W1 = jax.random.normal(k3, (E, D, F), dtype=jnp.float32) / np.sqrt(D)
        W2 = jax.random.normal(k4, (E, F, D), dtype=jnp.float32) / np.sqrt(F)
        return {'x': x, 'choice': choice, 'W1': W1, 'W2': W2}
    _L1_ffn_all = _L1_ffn_setup()
    _L1_ffn_in = {k: v for k, v in _L1_ffn_all.items() if k in ('choice', 'W1', 'W2')}
    del _L1_ffn_all
    return {'x': x, 'ctx_1024': ctx_1024, 'L0_xattn_Wq': _L0_xattn_in['Wq'], 'L0_xattn_Wk': _L0_xattn_in['Wk'], 'L0_xattn_Wv': _L0_xattn_in['Wv'], 'L0_xattn_Wo': _L0_xattn_in['Wo'], 'L0_xattn_bo': _L0_xattn_in['bo'], 'L0_ffn_scale': _L0_ffn_in['scale'], 'L0_ffn_gate_w': _L0_ffn_in['gate_w'], 'L0_ffn_gate_b': _L0_ffn_in['gate_b'], 'L0_ffn_mlp1_w': _L0_ffn_in['mlp1_w'], 'L0_ffn_mlp1_b': _L0_ffn_in['mlp1_b'], 'L0_ffn_mlp2_w': _L0_ffn_in['mlp2_w'], 'L0_ffn_mlp2_b': _L0_ffn_in['mlp2_b'], 'L1_xattn_Wq': _L1_xattn_in['Wq'], 'L1_xattn_Wk': _L1_xattn_in['Wk'], 'L1_xattn_Wv': _L1_xattn_in['Wv'], 'L1_xattn_Wo': _L1_xattn_in['Wo'], 'L1_xattn_bo': _L1_xattn_in['bo'], 'L1_ffn_choice': _L1_ffn_in['choice'], 'L1_ffn_W1': _L1_ffn_in['W1'], 'L1_ffn_W2': _L1_ffn_in['W2']}

def reference(x, ctx_1024, L0_xattn_Wq, L0_xattn_Wk, L0_xattn_Wv, L0_xattn_Wo, L0_xattn_bo, L0_ffn_scale, L0_ffn_gate_w, L0_ffn_gate_b, L0_ffn_mlp1_w, L0_ffn_mlp1_b, L0_ffn_mlp2_w, L0_ffn_mlp2_b, L1_xattn_Wq, L1_xattn_Wk, L1_xattn_Wv, L1_xattn_Wo, L1_xattn_bo, L1_ffn_choice, L1_ffn_W1, L1_ffn_W2):
    import jax
    import jax.numpy as jnp

    def _L0_xattn_ref(x, context, Wq, Wk, Wv, Wo, bo):
        import jax, jax.numpy as jnp
        import numpy as np
        DIM = 128
        NUM_HEADS = 8
        HEAD_DIM = 64
        INNER = NUM_HEADS * HEAD_DIM
        B, N, _ = x.shape
        M = context.shape[1]
        scale = HEAD_DIM ** (-0.5)
        q = (x @ Wq).reshape(B, N, NUM_HEADS, HEAD_DIM).transpose(0, 2, 1, 3)
        k = (context @ Wk).reshape(B, M, NUM_HEADS, HEAD_DIM).transpose(0, 2, 1, 3)
        v = (context @ Wv).reshape(B, M, NUM_HEADS, HEAD_DIM).transpose(0, 2, 1, 3)
        attn = jax.nn.softmax(jnp.einsum('bhnd,bhmd->bhnm', q, k) * scale, axis=-1)
        out = jnp.einsum('bhnm,bhmd->bhnd', attn, v)
        out = out.transpose(0, 2, 1, 3).reshape(B, N, INNER)
        return out @ Wo + bo

    def _L0_ffn_ref(x, scale, gate_w, gate_b, mlp1_w, mlp1_b, mlp2_w, mlp2_b):
        import jax, jax.numpy as jnp
        import numpy as np
        ALPHA = 1.702
        LIMIT = 7.0
        EPS = 1e-05
        E = 16
        K = 4

        def _swiglu(h):
            x_glu = jnp.minimum(h[..., ::2], LIMIT)
            x_lin = jnp.clip(h[..., 1::2], LIMIT, LIMIT)
            return x_glu * jax.nn.sigmoid(ALPHA * x_glu) * (x_lin + 1.0)
        t = x * jax.lax.rsqrt(jnp.mean(x * x, axis=-1, keepdims=True) + EPS) * scale
        g = jnp.einsum('bth,eh->bte', t, gate_w) + gate_b
        vals, idx = jax.lax.top_k(g, K)
        w = jax.nn.softmax(vals, axis=-1)
        route = jnp.sum(jax.nn.one_hot(idx, E, dtype=t.dtype) * w[..., None], axis=-2)
        route_e = jnp.moveaxis(route, -1, 0)

        def step(acc, p):
            w1, b1, w2, b2, r = p
            h = jnp.einsum('bth,ih->bti', t, w1) + b1
            s = _swiglu(h)
            y = jnp.einsum('bti,hi->bth', s, w2) + b2
            return (acc + r[..., None] * y, None)
        acc, _ = jax.lax.scan(step, jnp.zeros_like(x), (mlp1_w, mlp1_b, mlp2_w, mlp2_b, route_e))
        return x + acc

    def _L1_xattn_ref(query, key, value, Wq, Wk, Wv, Wo, bo):
        import jax, jax.numpy as jnp
        import numpy as np
        D_MODEL = 128
        NUM_HEADS = 16
        HEAD_DIM = D_MODEL // NUM_HEADS
        B, S, _ = query.shape

        def proj_split(x, W):
            y = jnp.einsum('bsd,ed->bse', x, W)
            return y.reshape(B, -1, NUM_HEADS, HEAD_DIM).transpose(0, 2, 1, 3)
        q = proj_split(query, Wq)
        k = proj_split(key, Wk)
        v = proj_split(value, Wv)
        scores = jnp.einsum('bhqd,bhkd->bhqk', q, k) / np.sqrt(HEAD_DIM)
        attn = jax.nn.softmax(scores, axis=-1)
        out = jnp.einsum('bhqk,bhkd->bhqd', attn, v)
        out = out.transpose(0, 2, 1, 3).reshape(B, -1, D_MODEL)
        return jnp.einsum('bsd,ed->bse', out, Wo) + bo

    def _L1_ffn_ref(x, choice, W1, W2):
        import jax, jax.numpy as jnp
        import numpy as np
        TOP_K = 2
        B, S, D = x.shape
        E = choice.shape[0]
        logits = jnp.einsum('bsd,ed->bse', x, choice)
        weights = jax.nn.softmax(logits, axis=-1)
        k_w, k_idx = jax.lax.top_k(weights, TOP_K)
        cw = jnp.sum(jax.nn.one_hot(k_idx, E, dtype=x.dtype) * k_w[..., None], axis=-2)
        xt = x.reshape(B * S, D)
        cwt = cw.reshape(B * S, E)
        y = jnp.zeros_like(xt)
        for e in range(E):
            h = jax.nn.silu(xt @ W1[e]) @ W2[e]
            y = y + cwt[:, e:e + 1] * h
        return y.reshape(B, S, D)
    x = x + _L0_xattn_ref(_layernorm(x, axis=-1), ctx_1024, L0_xattn_Wq, L0_xattn_Wk, L0_xattn_Wv, L0_xattn_Wo, L0_xattn_bo)
    x = x + _L0_ffn_ref(_layernorm(x, axis=-1), L0_ffn_scale, L0_ffn_gate_w, L0_ffn_gate_b, L0_ffn_mlp1_w, L0_ffn_mlp1_b, L0_ffn_mlp2_w, L0_ffn_mlp2_b)
    x = x + _L1_xattn_ref(_layernorm(x, axis=-1), ctx_1024, ctx_1024, L1_xattn_Wq, L1_xattn_Wk, L1_xattn_Wv, L1_xattn_Wo, L1_xattn_bo)
    x = x + _L1_ffn_ref(_layernorm(x, axis=-1), L1_ffn_choice, L1_ffn_W1, L1_ffn_W2)
    return x

_drawn_inputs = setup_inputs


def setup_inputs(seed=0):
    import zlib

    import numpy as np

    out = dict(_drawn_inputs(seed))
    spreads = {'L0_ffn_scale': (1.0, 0.6), 'L0_ffn_gate_b': (0.0, 0.1)}
    factors = {'L0_xattn_bo': 4.523, 'L0_ffn_mlp1_b': 8.0, 'L0_ffn_mlp2_b': 8.0}
    for name, (base, spread) in spreads.items():
        noise = np.random.default_rng([zlib.crc32(name.encode()), seed]).standard_normal(out[name].shape)
        drawn = base * np.exp(spread * noise) if base else spread * noise
        out[name] = jnp.asarray(drawn.astype(out[name].dtype))
    for name, factor in factors.items():
        out[name] = (out[name] * factor).astype(out[name].dtype)
    return out
```

```python
from contextlib import ExitStack

import concourse.bass as bass
from concourse import mybir

F32 = mybir.dt.float32
F32R = mybir.dt.float32r
ALU = mybir.AluOpType
ACT = mybir.ActivationFunctionType
AX = mybir.AxisListType

P = 128
D = 128
SEQ = 64
TILE = 512
SUBS = TILE // P
ROWS = TILE // SEQ
H0, DH0 = 8, 64
H1, DH1 = 16, 8
E0, K0 = 16, 4
E1, K1, F1 = 8, 2, 512
C1 = F1 // P
EPS = 1e-5
ALPHA, LIMIT = 1.702, 7.0
LOW = -3.0e38

COST = dict(k0=640, v0=900, k1=880, v1=900, T=500, S0=900, PT0=500, PV0=900, gate=500, rT=900, rb=900,
            h0=640, y0=870, q1=880, S1=1800, PT1=1000, PV1=1500, oT=500, wo=900, h1=640, y1=870)


def attention_and_first_experts():
    steps = [("ctx_split", 0), ("ln_stats", 1), ("ln_apply", 1)]
    for j in range(H0):
        steps += [("k0", j), ("v0", j)]
        if j == 3:
            steps += [("T", 1)]
    for j in range(SUBS + 3):
        if 0 <= j - 2 < SUBS:
            steps += [("PT0", j - 2)]
        if j < SUBS:
            steps += [("S0", j), ("sub0", j)]
        if 0 <= j - 1 < SUBS:
            steps += [("norm0", j - 1)]
        if 0 <= j - 3 < SUBS:
            steps += [("PV0", j - 3)]
    steps += [("res0", 0), ("ln_stats", 2), ("k1", 0), ("ln_apply", 2), ("T", 2), ("gate", 0)]
    steps += [("route_a", 0), ("h0", 0), ("route_b", 0), ("h0", 1), ("route_c", 0), ("s0", 0), ("rT", 0),
              ("rb", 0)]
    for e in range(2, E0 + 3):
        if e < E0:
            steps += [("h0", e)]
        if e - 1 < E0:
            steps += [("s0", e - 1)]
        if e - 2 < E0:
            steps += [("y0", e - 2)]
        if 0 <= e - 3 < E0:
            steps += [("acc0", e - 3)]
    steps += [("ln_stats", 3), ("ln_apply", 3), ("v1", 0), ("v1", 1), ("T", 3), ("q1", 0)]
    for j in range(SUBS + 3):
        if 0 <= j - 2 < SUBS:
            steps += [("PT1", j - 2)]
        if j < SUBS:
            steps += [("S1", j), ("sub1", j)]
        if 0 <= j - 1 < SUBS:
            steps += [("norm1", j - 1)]
        if 0 <= j - 3 < SUBS:
            steps += [("PV1", j - 3)]
    steps += [("oT", 0), ("wo", 0), ("res1", 0), ("ln_stats", 4), ("ln_apply", 4), ("T", 4), ("gate", 1),
              ("route_a", 1), ("route_b", 1), ("route_c", 1)]
    return steps


def second_experts():
    steps = []
    for j in range(E1 * C1 + 2):
        if j < E1 * C1:
            steps += [("h1", j), ("s1", j)]
        if j >= 2:
            steps += [("y1", j - 2)]
            if (j - 2) % C1 == C1 - 1:
                steps += [("acc1", (j - 2) // C1)]
    return steps + [("store", 0)]


def woven(a, b, lead):
    total_a = sum(COST.get(n, 0) for n, _ in a) - lead
    total_b = sum(COST.get(n, 0) for n, _ in b)
    out, done_a, done_b, at = [], -lead, 0, 0
    for name, j in a:
        out.append(("A", name, j))
        done_a += COST.get(name, 0)
        while at < len(b) and done_b * total_a <= done_a * total_b and done_a > 0:
            out.append(("B", *b[at]))
            done_b += COST.get(b[at][0], 0)
            at += 1
    return out + [("B", *s) for s in b[at:]]


A_STEPS = attention_and_first_experts()
B_STEPS = second_experts()
WOVEN = woven(A_STEPS, B_STEPS, 4000)


def banks_of(name, j):
    if name in ("k0", "h0"):
        return [j % 2]
    if name in ("v0", "y0"):
        return [2 + j % 2]
    if name == "v1":
        return [1 + j]
    if name in ("k1", "q1", "gate", "oT"):
        return [0]
    if name in ("rT", "wo"):
        return [1]
    if name == "rb":
        return [2]
    if name == "T":
        return [4]
    if name == "S0":
        return [j % 2]
    if name == "PT0":
        return [2 + j % 2]
    if name == "S1":
        return [0, 1]
    if name == "PT1":
        return [2, 3]
    if name in ("PV0", "PV1"):
        return [4] if j == SUBS - 1 else []
    if name == "h1":
        return [5 + j % 2]
    if name == "y1":
        return [7] if j % C1 == C1 - 1 else []
    return []


ROUTE_STEPS, POOL_STEPS = 8, 9

USES = {b: [s for s in A_STEPS + B_STEPS if b in banks_of(*s)] for b in range(8)}


def use(bank, name, j, t):
    return t * len(USES[bank]) + USES[bank].index((name, j)) + 1


def xffn_kernel(nc, x, ctxT, wq0T, wk0T, wv0T, wo0, bo0, scale0, gw0T, gb0, w10T, b10, w20T, b20,
                wq1T, wk1T, wv1T, wo1T, bo1, gw1T, w11, w21, out):
    TILES = x.shape[0]
    with ExitStack() as ctx:
        def sb(name, shape, dt=F32):
            return ctx.enter_context(nc.sbuf_tensor(name, shape, dt))

        def sem(name):
            return ctx.enter_context(nc.semaphore(name))

        A_hi = sb("A_hi", [P, H0, D], F32R)
        A_lo = sb("A_lo", [P, H0, D], F32R)
        Cw = sb("Cw", [P, 2, H0 // 2, D])
        w10_hi = sb("w10_hi", [P, E0, P], F32R)
        w10_lo = sb("w10_lo", [P, E0, P], F32R)
        w20 = sb("w20", [P, E0, D])
        w11_hi = sb("w11_hi", [P, E1 * C1, P], F32R)
        w11_lo = sb("w11_lo", [P, E1 * C1, P], F32R)
        w21_sb = sb("w21_sb", [P, E1 * C1, D])
        wq1 = sb("wq1", [P, D])
        wk1 = sb("wk1", [P, D])
        wv1 = sb("wv1", [P, 2, D])
        wo1 = sb("wo1", [P, D])
        gw0 = sb("gw0", [P, E0])
        gw1 = sb("gw1", [P, E1])
        b1c = sb("b1c", [P, E0])
        b2r = sb("b2r", [E0, D])
        scale_c = sb("scale_c", [P, 1])
        bo0_b = sb("bo0_b", [P, D])
        bo1_b = sb("bo1_b", [P, D])
        gb0_b = sb("gb0_b", [P, E0])
        ident = sb("ident", [P, P])
        eps_c = sb("eps_c", [P, SUBS])
        minus_half = sb("minus_half", [P, SUBS])
        ctx_t = sb("ctx_t", [P, TILE])
        op_hi = sb("op_hi", [P, TILE], F32R)
        op_lo = sb("op_lo", [P, TILE], F32R)
        in1_hi = sb("in1_hi", [P, TILE], F32R)
        in1_lo = sb("in1_lo", [P, TILE], F32R)
        x_in = sb("x_in", [P, SUBS, D])
        x1 = sb("x1", [P, SUBS, D])
        x3 = sb("x3", [P, SUBS, D])
        acc = sb("acc", [P, SUBS, D])
        z = sb("z", [P, SUBS, D])
        tz = sb("tz", [P, SUBS, D])
        zT = sb("zT", [P, TILE])
        kp = sb("kp", [P, H0, TILE])
        vp = sb("vp", [P, ROWS, TILE])
        Kb = sb("Kb", [P, H1, TILE])
        ex = sb("ex", [P, 2, 2 * TILE])
        pt = sb("pt", [P, 2, 2 * TILE])
        th1 = sb("th1", [P, 2, TILE])
        s1 = sb("s1", [P, 3, TILE])
        g0, th0, s0 = vp[:, 0:2, :], vp[:, 2:4, :], vp[:, 4:6, :]
        V1, qT, o1 = kp[:, 0:2, :], kp[:, 2, :], kp[:, 3, :]
        oT, kT = kp[:, 4, :], vp[:, 6, :]
        rT = vp[0:E0, 7, :]
        raw11, raw10 = Kb[:, 0:8, :], Kb[:, 8:12, :]
        st = sb("st", [P, SUBS, 6])
        mv = sb("mv", [P, SUBS, 2])
        ve = sb("ve", [P, SUBS])
        rstd = sb("rstd", [P, SUBS])
        ms = sb("ms", [P, SUBS])
        rt = sb("rt", [P, SUBS])
        mx = sb("mx", [P, 2, H1])
        sm = sb("sm", [P, 2, H1])
        ri = sb("ri", [P, 2, H1])
        gl0 = sb("gl0", [P, SUBS, E0 + 8 - K0])
        gl1 = sb("gl1", [P, SUBS, E1 + 8 - K1])
        m8 = sb("m8", [P, SUBS, 8])
        mt0 = sb("mt0", [P, SUBS, 8])
        mt1 = sb("mt1", [P, SUBS, 8])
        rep = sb("rep", [P, SUBS, E0 + 8])
        gd = sb("gd", [P, SUBS, E0])
        msk = sb("msk", [P, SUBS, E0])
        gs = sb("gs", [P, SUBS])
        gr = sb("gr", [P, SUBS])
        r0 = sb("r0", [P, SUBS, E0])
        r1 = sb("r1", [P, SUBS, E1])

        ps01 = ctx.enter_context(nc.psum_tensor("ps01", [P, 2, TILE], F32))
        ps23 = ctx.enter_context(nc.psum_tensor("ps23", [P, 2, TILE], F32))
        ps4 = ctx.enter_context(nc.psum_tensor("ps4", [P, TILE], F32))
        ps56 = ctx.enter_context(nc.psum_tensor("ps56", [P, 2, TILE], F32))
        ps7 = ctx.enter_context(nc.psum_tensor("ps7", [P, TILE], F32))
        BANK = [ps01[:, 0, :], ps01[:, 1, :], ps23[:, 0, :], ps23[:, 1, :], ps4[:, :],
                ps56[:, 0, :], ps56[:, 1, :], ps7[:, :]]

        full = [sem(f"full{b}") for b in range(8)]
        free = [sem(f"free{b}") for b in range(8)]
        loaded = {n: sem(f"loaded_{n}") for n in ("qk0", "vo0", "w1s", "w10", "w11", "small", "w20", "w21")}
        x_loaded, ctx_loaded, stored = sem("x_loaded"), sem("ctx_loaded"), sem("stored")
        banded = sem("banded")
        pool_drained = sem("pool_drained")
        waited_apart = sem("waited_apart")
        consts = sem("consts")
        prep_products = sem("prep_products")
        prep_a = sem("prep_a")
        prep_v = sem("prep_v")
        prep_g = sem("prep_g")
        bn_done = sem("bn_done")
        var_ready = sem("var_ready")
        pool_step = sem("pool_step")
        rstd_ready = sem("rstd_ready")
        z_ready = sem("z_ready")
        hi_done = sem("hi_done")
        split_ready = sem("split_ready")
        bias_added = sem("bias_added")
        max_done = sem("max_done")
        exp_done = sem("exp_done")
        sum_done = sem("sum_done")
        inv_done = sem("inv_done")
        prob_ready = sem("prob_ready")
        x1z_ready = sem("x1z_ready")
        route_step = sem("route_step")
        gexp_done = sem("gexp_done")
        route_ready = sem("route_ready")
        x3_ready = sem("x3_ready")
        th0_ready = sem("th0_ready")
        s0_ready = sem("s0_ready")
        th1_ready = sem("th1_ready")

        SOFT = 2 * SUBS

        def at_least(eng, s, value):
            if not isinstance(value, int) or value > 0:
                eng.wait_ge(s, value)

        def wait_full(eng, b, name, j, t):
            eng.wait_ge(full[b], use(b, name, j, t))

        def wait_emptied(eng, b, name, j, t):
            at_least(eng, free[b], use(b, name, j, t))

        def wait_free(eng, b, name, j, t):
            at_least(eng, free[b], use(b, name, j, t) - 1)

        def wait_apart(eng, s, value):
            eng.wait_ge(s, value)
            eng.sem_inc(waited_apart, 1)

        def first(t):
            return isinstance(t, int) and t == 0

        def one(t):
            return slice(t, t + 1) if isinstance(t, int) else bass.ds(t, 1)

        def tiles(eng, step):
            for name, j in A_STEPS:
                step(name, j, 0)
            for part, name, j in WOVEN:
                step(name, j, 1 if part == "A" else 0)
            with eng.Fori(1, TILES - 2) as i:
                for part, name, j in WOVEN:
                    step(name, j, i + 1 if part == "A" else i)
            for part, name, j in WOVEN:
                step(name, j, TILES - 1 if part == "A" else TILES - 2)
            for name, j in B_STEPS:
                step(name, j, TILES - 1)

        block = ctx.enter_context(nc.Block())

        @block.sync
        def _(sp):
            def load_tile(t):
                sp.dma_start(ctx_t[:, :], ctxT[one(t)].rearrange("o p n -> (o p) n")).then_inc(ctx_loaded, 16)
                sp.dma_start(x_in[:, :, :], x[one(t)].rearrange("o p s d -> (o p) s d")).then_inc(x_loaded, 16)

            sp.dma_start(ex[0:DH0, 0, :], wk0T).then_inc(loaded["qk0"], 16)
            sp.dma_start(ex[0:DH0, 1, :], wq0T).then_inc(loaded["qk0"], 16)
            sp.dma_start(pt[0:DH0, 0, :], wv0T).then_inc(loaded["vo0"], 16)
            sp.dma_start(pt[0:DH0, 1, :], wo0).then_inc(loaded["vo0"], 16)
            load_tile(0)
            for dst, src in ((gw0, gw0T), (gw1, gw1T), (b1c, b10), (b2r, b20), (scale_c, scale0)):
                sp.dma_start(dst[:, :], src).then_inc(loaded["small"], 16)
            for dst, src in ((bo0_b, bo0), (bo1_b, bo1), (gb0_b, gb0)):
                sp.dma_start(dst[:, :], src.broadcast_to([P, src.shape[1]])).then_inc(loaded["small"], 16)
            for dst, src in ((wq1, wq1T), (wk1, wk1T), (wo1, wo1T)):
                sp.dma_start(dst[:, :], src).then_inc(loaded["w1s"], 16)
            for r in range(2):
                sp.dma_start(wv1[:, r, :], wv1T).then_inc(loaded["w1s"], 16)
            sp.dma_start(raw10, w10T).then_inc(loaded["w10"], 16)
            sp.dma_start(raw11, w11).then_inc(loaded["w11"], 16)
            sp.dma_start(w20[:, :, :], w20T).then_inc(loaded["w20"], 16)
            sp.dma_start(w21_sb[:, :, :], w21).then_inc(loaded["w21"], 16)

            def step(name, j, t):
                if name == "k1":
                    wait_emptied(sp, 0, name, j, t)
                    if first(t):
                        sp.wait_ge(prep_g, 3)
                    for h in range(H1):
                        rows = slice(DH1 * h, DH1 * h + DH1)
                        sp.dma_start(Kb[rows, h, :], kT[rows, :]).then_inc(banded, 16)
                elif name == "v1" and j == 1 and not (isinstance(t, int) and t == TILES - 1):
                    wait_emptied(sp, 2, name, j, t)
                    load_tile(t + 1)
                elif name == "store":
                    wait_emptied(sp, 7, "y1", E1 * C1 - 1, t)
                    sp.dma_start(out[one(t)].rearrange("o p s d -> (o p) s d"), acc[:, :, :]).then_inc(stored, 16)

            tiles(sp, step)
            sp.wait_ge(stored, 16 * TILES)

        @block.tensor
        def _(pe):
            def mm3(dst, l_hi, l_lo, r_hi, r_lo):
                pe.matmul(dst, l_hi, r_lo, start=True, stop=False)
                pe.matmul(dst, l_lo, r_hi, start=False, stop=False)
                return pe.matmul(dst, l_hi, r_hi, start=False, stop=True)

            pe.wait_ge(loaded["qk0"], 32)
            for h in range(H0):
                cols = slice(P * h, P * h + P)
                mm = pe.matmul(BANK[h // 4][:, P * (h % 4):P * (h % 4) + P], ex[0:DH0, 0, cols], ex[0:DH0, 1, cols],
                               start=True, stop=True, skip_group_check=True)
            mm.then_inc(prep_products, 1)
            pe.wait_ge(loaded["vo0"], 32)
            for h in range(H0):
                cols = slice(P * h, P * h + P)
                mm = pe.matmul(BANK[2 + h % 2][:, P * (h // 2):P * (h // 2) + P], pt[0:DH0, 0, cols],
                               pt[0:DH0, 1, cols], start=True, stop=True, skip_group_check=True)
            mm.then_inc(prep_products, 1)
            pe.wait_ge(consts, 1)

            def step(name, j, t):
                if name == "k0":
                    b = j % 2
                    if j == 0:
                        pe.wait_ge(split_ready, 3 * t + 1)
                        if first(t):
                            pe.wait_ge(prep_v, 1)
                    wait_free(pe, b, name, j, t)
                    mm3(BANK[b], A_hi[:, j, :], A_lo[:, j, :], op_hi[:, :], op_lo[:, :]).then_inc(full[b], 1)
                elif name == "v0":
                    b = 2 + j % 2
                    if first(t) and j == 0:
                        pe.wait_ge(prep_a, 2)
                    wait_free(pe, b, name, j, t)
                    row = ctx_t[:, SEQ * j:SEQ * j + SEQ]
                    pe.matmul(BANK[b][0:SEQ, :], row, Cw[:, 0, :, :], start=True, stop=True)
                    pe.matmul(BANK[b][SEQ:P, :], row, Cw[:, 1, :, :], start=True, stop=True).then_inc(full[b], 1)
                elif name == "k1":
                    if first(t):
                        pe.wait_ge(loaded["w1s"], 80)
                    wait_free(pe, 0, name, j, t)
                    pe.matmul(BANK[0], wk1[:, :], ctx_t[:, :], start=True, stop=True).then_inc(full[0], 1)
                elif name == "T":
                    pe.wait_ge(z_ready, 4 * t + j)
                    wait_free(pe, 4, name, j, t)
                    src = tz if j == 2 else z
                    for s in range(SUBS):
                        mm = pe.transpose(BANK[4][:, P * s:P * s + P], src[:, s, :], ident[:, :])
                    mm.then_inc(full[4], 1)
                elif name == "S0":
                    b = j % 2
                    if j == 0:
                        wait_emptied(pe, 4, "T", 1, t)
                        wait_emptied(pe, 1, "k0", H0 - 1, t)
                    wait_free(pe, b, name, j, t)
                    for r in range(2):
                        tok = slice(P * j + SEQ * r, P * j + SEQ * r + SEQ)
                        mm = pe.matmul(BANK[b][SEQ * r:SEQ * r + SEQ, :], zT[:, tok], kp[:, :, tok],
                                       start=True, stop=True)
                    mm.then_inc(full[b], 1)
                elif name == "PT0":
                    b = 2 + j % 2
                    pe.wait_ge(prob_ready, SOFT * t + j + 1)
                    wait_free(pe, b, name, j, t)
                    for i in range(H0 // 2):
                        mm = pe.transpose(BANK[b][:, P * i:P * i + P], ex[:, j % 2, P * i:P * i + P], ident[:, :])
                    mm.then_inc(full[b], 1)
                elif name == "PV0":
                    wait_emptied(pe, 2 + j % 2, "PT0", j, t)
                    if j == 0:
                        wait_free(pe, 4, name, SUBS - 1, t)
                    for i in range(H0 // 2):
                        for r in range(2):
                            mm = pe.matmul(BANK[4][SEQ * r:SEQ * r + SEQ, P * j:P * j + P],
                                           pt[:, j % 2, P * i + SEQ * r:P * i + SEQ * r + SEQ],
                                           vp[:, 2 * j + r, P * i:P * i + P],
                                           start=(i == 0), stop=(i == H0 // 2 - 1), skip_group_check=True)
                    if j == SUBS - 1:
                        mm.then_inc(full[4], 1)
                elif name == "gate":
                    wait_emptied(pe, 4, "T", 4 if j else 2, t)
                    wait_free(pe, 0, name, j, t)
                    if first(t) and j == 0:
                        pe.wait_ge(loaded["small"], 128)
                    n = E1 if j else E0
                    for s in range(SUBS):
                        mm = pe.matmul(BANK[0][:, n * s:n * s + n], zT[:, P * s:P * s + P],
                                       gw1[:, :] if j else gw0[:, :], start=True, stop=True, skip_group_check=True)
                    mm.then_inc(full[0], 1)
                elif name == "rT":
                    pe.wait_ge(route_ready, 2 * t + 1)
                    wait_free(pe, 1, name, j, t)
                    for s in range(SUBS):
                        mm = pe.transpose(BANK[1][0:E0, P * s:P * s + P], r0[:, s, :], ident[:, :])
                    mm.then_inc(full[1], 1)
                elif name == "rb":
                    wait_emptied(pe, 1, "rT", 0, t)
                    wait_free(pe, 2, name, j, t)
                    for s in range(SUBS):
                        mm = pe.matmul(BANK[2][:, P * s:P * s + P], rT[:, P * s:P * s + P], b2r[:, :],
                                       start=True, stop=True, skip_group_check=True)
                    mm.then_inc(full[2], 1)
                elif name == "h0":
                    b = j % 2
                    if j == 0:
                        pe.wait_ge(split_ready, 3 * t + 2)
                        if first(t):
                            pe.wait_ge(prep_g, 2)
                    wait_free(pe, b, name, j, t)
                    mm3(BANK[b], w10_hi[:, j, :], w10_lo[:, j, :], op_hi[:, :], op_lo[:, :]).then_inc(full[b], 1)
                elif name == "y0":
                    b = 2 + j % 2
                    pe.wait_ge(s0_ready, E0 * t + j + 1)
                    wait_free(pe, b, name, j, t)
                    if first(t) and j == 0:
                        pe.wait_ge(prep_a, 3)
                    for s in range(SUBS):
                        mm = pe.matmul(BANK[b][:, P * s:P * s + P], s0[:, j % 2, P * s:P * s + P], w20[:, j, :],
                                       start=True, stop=True, skip_group_check=True)
                    mm.then_inc(full[b], 1)
                elif name == "v1":
                    wait_free(pe, 1 + j, name, j, t)
                    if first(t) and j == 0:
                        pe.wait_ge(prep_v, 4)
                    for n in range(ROWS // 2):
                        tok = slice(SEQ * (4 * j + n), SEQ * (4 * j + n) + SEQ)
                        for r in range(2):
                            mm = pe.matmul(BANK[1 + j][SEQ * r:SEQ * r + SEQ, P * n:P * n + P], ctx_t[:, tok],
                                           wv1[:, r, :], start=True, stop=True, skip_group_check=True)
                    mm.then_inc(full[1 + j], 1)
                elif name == "q1":
                    wait_emptied(pe, 4, "T", 3, t)
                    wait_free(pe, 0, name, j, t)
                    pe.matmul(BANK[0], wq1[:, :], zT[:, :], start=True, stop=True).then_inc(full[0], 1)
                elif name == "S1":
                    if j == 0:
                        wait_emptied(pe, 0, "q1", 0, t)
                        pe.wait_ge(banded, 16 * H1 * (t + 1))
                    for b in range(2):
                        wait_free(pe, b, name, j, t)
                        for r in range(2):
                            tok = slice(P * j + SEQ * r, P * j + SEQ * r + SEQ)
                            mm = pe.matmul(BANK[b][SEQ * r:SEQ * r + SEQ, :], qT[:, tok], Kb[:, 8 * b:8 * b + 8, tok],
                                           start=True, stop=True)
                        mm.then_inc(full[b], 1)
                elif name == "PT1":
                    pe.wait_ge(prob_ready, SOFT * t + SUBS + j + 1)
                    for b in (2, 3):
                        wait_free(pe, b, name, j, t)
                        for i in range(4):
                            col = P * (4 * (b - 2) + i)
                            mm = pe.transpose(BANK[b][:, P * i:P * i + P], ex[:, j % 2, col:col + P], ident[:, :])
                        mm.then_inc(full[b], 1)
                elif name == "PV1":
                    wait_emptied(pe, 3, "PT1", j, t)
                    if j == 0:
                        wait_free(pe, 4, name, SUBS - 1, t)
                    for i in range(H1 // 2):
                        for r in range(2):
                            row = 2 * j + r
                            col = P * (row % 4) + 16 * i
                            mm = pe.matmul(BANK[4][SEQ * r:SEQ * r + SEQ, P * j + 16 * i:P * j + 16 * i + 16],
                                           pt[:, j % 2, P * i + SEQ * r:P * i + SEQ * r + SEQ],
                                           V1[:, row // 4, col:col + 16], start=True, stop=True,
                                           skip_group_check=True)
                    if j == SUBS - 1:
                        mm.then_inc(full[4], 1)
                elif name == "oT":
                    wait_emptied(pe, 4, "PV1", SUBS - 1, t)
                    wait_free(pe, 0, name, j, t)
                    for s in range(SUBS):
                        mm = pe.transpose(BANK[0][:, P * s:P * s + P], o1[:, P * s:P * s + P], ident[:, :])
                    mm.then_inc(full[0], 1)
                elif name == "wo":
                    wait_emptied(pe, 0, "oT", 0, t)
                    wait_free(pe, 1, name, j, t)
                    for s in range(SUBS):
                        mm = pe.matmul(BANK[1][:, P * s:P * s + P], oT[:, P * s:P * s + P], wo1[:, :],
                                       start=True, stop=True, skip_group_check=True)
                    mm.then_inc(full[1], 1)
                elif name == "h1":
                    b = 5 + j % 2
                    if j == 0:
                        pe.wait_ge(split_ready, 3 * t + 3)
                    wait_free(pe, b, name, j, t)
                    mm3(BANK[b], w11_hi[:, j, :], w11_lo[:, j, :], in1_hi[:, :], in1_lo[:, :]).then_inc(full[b], 1)
                elif name == "y1":
                    c = j % C1
                    wait_emptied(pe, 5 + j % 2, "h1", j, t)
                    if c == 0:
                        wait_free(pe, 7, name, j + C1 - 1, t)
                    if first(t) and j == 0:
                        pe.wait_ge(prep_a, 4)
                    for s in range(SUBS):
                        mm = pe.matmul(BANK[7][:, P * s:P * s + P], s1[:, j % 3, P * s:P * s + P], w21_sb[:, j, :],
                                       start=(c == 0 and s == 0), stop=(c == C1 - 1), skip_group_check=True)
                    if c == C1 - 1:
                        mm.then_inc(full[7], 1)

            tiles(pe, step)

        @block.scalar
        def _(act):
            act.wait_ge(prep_products, 1)
            act.activation(A_hi[:, :, :], ps01[:, :, :].rearrange("p a (b d) -> p (a b) d", d=D), ACT.Copy,
                           scale=DH0 ** -0.5).then_inc(prep_a, 1)
            act.wait_ge(prep_products, 2)
            act.activation(Cw[:, :, :, :], ps23[:, :, :].rearrange("p a (b d) -> p a b d", d=D),
                           ACT.Copy).then_inc(prep_a, 1)

            def copy_out(b, dst, name, j, t, **how):
                wait_full(act, b, name, j, t)
                act.activation(dst, BANK[b], ACT.Copy, **how).then_inc(free[b], 1)

            def step(name, j, t):
                if name == "k0":
                    copy_out(j % 2, kp[:, j, :], name, j, t)
                elif name == "v0":
                    copy_out(2 + j % 2, vp[:, j, :], name, j, t)
                elif name == "k1":
                    copy_out(0, kT, name, j, t)
                    if first(t):
                        act.wait_ge(loaded["w20"], 16)
                        act.activation(w20[:, :, :], w20[:, :, :], ACT.Copy,
                                       scale=(LIMIT + 1.0) / 2).then_inc(prep_a, 1)
                        act.wait_ge(loaded["w21"], 16)
                        act.activation(w21_sb[:, :, :], w21_sb[:, :, :], ACT.Copy, scale=0.5).then_inc(prep_a, 1)
                elif name == "T":
                    if j == 1:
                        at_least(act, split_ready, 3 * t)
                    copy_out(4, zT[:, :], name, j, t, **({"scale": scale_c[:, 0:1]} if j == 2 else {}))
                elif name in ("sub0", "sub1"):
                    n = j % 2
                    if name == "sub0":
                        wait_emptied(act, n, "S0", j, t)
                        e = ex[:, n, 0:TILE]
                    else:
                        wait_emptied(act, 1, "S1", j, t)
                        e = ex[:, n, :]
                    act.activation(e, e, ACT.Exp).then_inc(exp_done, 1)
                elif name == "PT0":
                    copy_out(2 + j % 2, pt[:, j % 2, 0:TILE], name, j, t)
                elif name == "PT1":
                    for b in (2, 3):
                        copy_out(b, pt[:, j % 2, TILE * (b - 2):TILE * (b - 1)], name, j, t)
                elif name == "route_b":
                    n = E1 if j else E0
                    act.wait_ge(route_step, ROUTE_STEPS * (2 * t + j) + 3)
                    act.activation(gd[:, :, 0:n], gd[:, :, 0:n], ACT.Exp).then_inc(gexp_done, 1)
                elif name == "rT":
                    wait_full(act, 1, name, j, t)
                    act.activation(rT, BANK[1][0:E0, :], ACT.Copy).then_inc(free[1], 1)
                elif name == "h0":
                    wait_emptied(act, j % 2, name, j, t)
                    act.activation(th0[:, j % 2, :], g0[:, j % 2, :], ACT.Tanh, scale=ALPHA / 2)\
                       .then_inc(th0_ready, 1)
                elif name == "v1":
                    copy_out(1 + j, V1[:, j, :], name, j, t)
                elif name == "q1":
                    copy_out(0, qT, name, j, t, scale=DH1 ** -0.5)
                elif name == "PV1" and j == SUBS - 1:
                    copy_out(4, o1, name, j, t)
                elif name == "oT":
                    copy_out(0, oT, name, j, t)
                elif name == "h1":
                    wait_full(act, 5 + j % 2, name, j, t)
                    act.activation(th1[:, j % 2, :], BANK[5 + j % 2], ACT.Tanh, scale=0.5).then_inc(th1_ready, 1)

            tiles(act, step)

        @block.vector
        def _(dve):
            dve.wait_ge(prep_a, 1)
            dve.scalar_tensor_tensor(out=A_lo[:, :, :], in0=ps01[:, :, :].rearrange("p a (b d) -> p (a b) d", d=D),
                                     scalar=DH0 ** -0.5, in1=A_hi[:, :, :].bitcast(F32), op0=ALU.mult,
                                     op1=ALU.subtract).then_inc(prep_v, 1)

            def softmax_shift(b, heads, e, name, j, t, n):
                wait_full(dve, b, name, j, t)
                s = BANK[b].rearrange("p (h m) -> p h m", h=8)
                m = mx[:, j % 2, 8 * (b if heads == H1 else 0):][:, 0:8]
                dve.tensor_reduce(m, s, AX.X, ALU.max).then_inc(max_done, 1)
                dve.wait_ge(max_done, n)
                dve.tensor_tensor(e.rearrange("p (h m) -> p h m", h=8), s,
                                  m.unsqueeze(2).to_broadcast([P, 8, SEQ]), ALU.subtract).then_inc(free[b], 1)

            def step(name, j, t):
                if name == "ln_stats":
                    src = x_in if j == 1 else x1 if j < 4 else x3
                    if j == 1:
                        dve.wait_ge(x_loaded, 16 * t + 16)
                    elif j == 2:
                        wait_emptied(dve, 4, "PV0", SUBS - 1, t)
                    elif j == 3:
                        wait_emptied(dve, 3, "y0", E0 - 1, t)
                    else:
                        wait_emptied(dve, 1, "wo", 0, t)
                    for s in range(SUBS):
                        ins = dve.bn_stats(st[:, s, :], src[:, s, :])
                    ins.then_inc(bn_done, 1)
                    wait_apart(dve, bn_done, 4 * t + j)
                    for s in range(SUBS):
                        ins = dve.bn_aggr(mv[:, s, :], st[:, s, :])
                    ins.then_inc(var_ready, 1)
                elif name == "ln_apply":
                    src = x_in if j == 1 else x1 if j < 4 else x3
                    dve.wait_ge(rstd_ready, 4 * t + j)
                    if j == 3:
                        dve.wait_ge(x1z_ready, t + 1)
                    for s in range(SUBS):
                        ins = dve.tensor_scalar(z[:, s, :], src[:, s, :], mv[:, s, 0:1], rstd[:, s:s + 1],
                                                ALU.subtract, ALU.mult)
                    if j == 2:
                        for s in range(SUBS):
                            ins = dve.tensor_scalar(tz[:, s, :], src[:, s, :], mv[:, s, 0:1], rt[:, s:s + 1],
                                                    ALU.subtract, ALU.mult)
                    ins.then_inc(z_ready, 1)
                    if first(t) and j == 1:
                        dve.wait_ge(loaded["w11"], 16)
                        raw = raw11.rearrange("p a (b f) -> p (a b) f", f=P)
                        dve.tensor_copy(w11_hi[:, :, :], raw).then_inc(prep_v, 1)
                        dve.wait_ge(prep_v, 2)
                        dve.tensor_tensor(w11_lo[:, :, :], raw, w11_hi[:, :, :].bitcast(F32),
                                          ALU.subtract).then_inc(prep_v, 1)
                        dve.wait_ge(loaded["w1s"], 80)
                        for r in range(2):
                            pairs = wv1[:, r, :].rearrange("p (i r d) -> p i r d", r=2, d=DH1)
                            ins = dve.memset(pairs[:, :, 1 - r, :], 0.0)
                        ins.then_inc(prep_v, 1)
                elif name == "sub0":
                    softmax_shift(j % 2, H0, ex[:, j % 2, 0:TILE], "S0", j, t, 3 * SUBS * t + j + 1)
                elif name == "sub1":
                    for b in range(2):
                        softmax_shift(b, H1, ex[:, j % 2, TILE * b:TILE * b + TILE], "S1", j, t,
                                      3 * SUBS * t + SUBS + 2 * j + b + 1)
                elif name in ("norm0", "norm1"):
                    h, k = (H0, j) if name == "norm0" else (H1, SUBS + j)
                    n = SOFT * t + k + 1
                    dve.wait_ge(exp_done, n)
                    dve.tensor_reduce(sm[:, j % 2, 0:h], ex[:, j % 2, 0:SEQ * h].rearrange("p (h m) -> p h m", h=h),
                                      AX.X, ALU.add).then_inc(sum_done, 1)
                    dve.wait_ge(sum_done, n)
                    dve.reciprocal(ri[:, j % 2, 0:h], sm[:, j % 2, 0:h]).then_inc(inv_done, 1)
                elif name == "res0":
                    wait_full(dve, 4, "PV0", SUBS - 1, t)
                    dve.wait_ge(bias_added, 2 * t + 1)
                    flat = x1[:, :, :].rearrange("p s d -> p (s d)")
                    dve.tensor_tensor(flat, BANK[4], flat, ALU.add).then_inc(free[4], 1)
                elif name == "res1":
                    wait_full(dve, 1, "wo", 0, t)
                    dve.wait_ge(bias_added, 2 * t + 2)
                    flat = x3[:, :, :].rearrange("p s d -> p (s d)")
                    dve.tensor_tensor(flat, BANK[1], flat, ALU.add).then_inc(free[1], 1)
                elif name == "rb":
                    wait_full(dve, 2, name, j, t)
                    dve.wait_ge(x1z_ready, t + 1)
                    flat = x1[:, :, :].rearrange("p s d -> p (s d)")
                    dve.tensor_tensor(flat, BANK[2], flat, ALU.add).then_inc(free[2], 1)
                elif name == "route_a":
                    n, k, gl, mt = (E1, K1, gl1, mt1) if j else (E0, K0, gl0, mt0)
                    r = ROUTE_STEPS * (2 * t + j)
                    wait_full(dve, 0, "gate", j, t)
                    got = BANK[0][:, 0:SUBS * n].rearrange("p (s e) -> p s e", s=SUBS)
                    if j:
                        dve.tensor_copy(gl[:, :, 0:n], got).then_inc(free[0], 1)
                    else:
                        dve.tensor_tensor(gl[:, :, 0:n], got, gb0_b[:, :].unsqueeze(1).to_broadcast([P, SUBS, n]),
                                          ALU.add).then_inc(free[0], 1)
                    dve.wait_ge(consts, 1)
                    wait_emptied(dve, 0, "gate", j, t)
                    for s in range(SUBS):
                        ins = dve.max(m8[:, s, :], gl[:, s, 0:n])
                    ins.then_inc(route_step, 1)
                    dve.wait_ge(route_step, r + 1)
                    dve.tensor_copy(mt[:, :, 0:k], m8[:, :, 0:k]).then_inc(route_step, 1)
                    dve.tensor_tensor(gd[:, :, 0:n], gl[:, :, 0:n], m8[:, :, 0:1].to_broadcast([P, SUBS, n]),
                                      ALU.subtract).then_inc(route_step, 1)
                elif name == "route_b":
                    n, k, gl, mt = (E1, K1, gl1, mt1) if j else (E0, K0, gl0, mt0)
                    r = ROUTE_STEPS * (2 * t + j)
                    width = n + 8 - k
                    wait_apart(dve, route_step, r + 2)
                    for s in range(SUBS):
                        ins = dve.match_replace(rep[:, s, 0:width], mt[:, s, :], gl[:, s, :], LOW)
                    ins.then_inc(route_step, 1)
                    dve.wait_ge(route_step, r + 4)
                    dve.tensor_tensor(msk[:, :, 0:n], rep[:, :, 0:n], gl[:, :, 0:n],
                                      ALU.not_equal).then_inc(route_step, 1)
                elif name == "route_c":
                    n, rr = (E1, r1) if j else (E0, r0)
                    r = ROUTE_STEPS * (2 * t + j)
                    dve.wait_ge(gexp_done, 2 * t + j + 1)
                    dve.wait_ge(route_step, r + 5)
                    dve.tensor_tensor(msk[:, :, 0:n], gd[:, :, 0:n], msk[:, :, 0:n], ALU.mult).then_inc(route_step, 1)
                    if not j:
                        dve.wait_ge(route_step, r + 6)
                    dve.tensor_reduce(gs[:, :], (gd if j else msk)[:, :, 0:n], AX.X, ALU.add).then_inc(route_step, 1)
                    dve.wait_ge(route_step, r + 7)
                    dve.reciprocal(gr[:, :], gs[:, :]).then_inc(route_step, 1)
                    dve.wait_ge(route_step, r + 8)
                    dve.tensor_tensor(rr[:, :, :], msk[:, :, 0:n], gr[:, :].unsqueeze(2).to_broadcast([P, SUBS, n]),
                                      ALU.mult).then_inc(route_ready, 1)
                elif name == "h0":
                    b = j % 2
                    if j >= 2:
                        dve.wait_ge(s0_ready, E0 * t + j - 1)
                    wait_full(dve, b, name, j, t)
                    dve.tensor_scalar(g0[:, b, :], BANK[b], b1c[:, j:j + 1], LIMIT, ALU.add,
                                      ALU.min).then_inc(free[b], 1)
                elif name == "s0":
                    if j >= 2:
                        wait_full(dve, 2 + j % 2, "y0", j - 2, t)
                    dve.wait_ge(th0_ready, E0 * t + j + 1)
                    dve.scalar_tensor_tensor(out=s0[:, j % 2, :], in0=th0[:, j % 2, :], scalar=1.0,
                                             in1=g0[:, j % 2, :], op0=ALU.add, op1=ALU.mult).then_inc(s0_ready, 1)
                elif name == "acc0":
                    b = 2 + j % 2
                    if j:
                        wait_emptied(dve, 5 - b, "y0", j - 1, t)
                    else:
                        wait_emptied(dve, 2, "rb", 0, t)
                        dve.wait_ge(route_ready, 2 * t + 1)
                    wait_full(dve, b, "y0", j, t)
                    for s in range(SUBS):
                        ins = dve.scalar_tensor_tensor(out=x1[:, s, :], in0=BANK[b][:, P * s:P * s + P],
                                                       scalar=r0[:, s, j:j + 1], in1=x1[:, s, :],
                                                       op0=ALU.mult, op1=ALU.add)
                    ins.then_inc(free[b], 1)
                elif name == "s1":
                    b = 5 + j % 2
                    dve.wait_ge(th1_ready, E1 * C1 * t + j + 1)
                    dve.scalar_tensor_tensor(out=s1[:, j % 3, :], in0=th1[:, j % 2, :], scalar=1.0, in1=BANK[b],
                                             op0=ALU.add, op1=ALU.mult).then_inc(free[b], 1)
                elif name == "acc1":
                    last = C1 * j + C1 - 1
                    if j:
                        wait_emptied(dve, 7, "y1", last - C1, t)
                    else:
                        dve.wait_ge(route_ready, 2 * t + 2)
                        at_least(dve, stored, 16 * t)
                    wait_full(dve, 7, "y1", last, t)
                    for s in range(SUBS):
                        ins = dve.scalar_tensor_tensor(out=acc[:, s, :], in0=BANK[7][:, P * s:P * s + P],
                                                       scalar=r1[:, s, j:j + 1], in1=(acc if j else x3)[:, s, :],
                                                       op0=ALU.mult, op1=ALU.add)
                    ins.then_inc(free[7], 1)

            tiles(dve, step)

        @block.gpsimd
        def _(pool):
            pool.memset(ident[:, :], 0.0)
            pool.memset(eps_c[:, :], EPS)
            pool.memset(minus_half[:, :], -0.5)
            for gl, mt, n, k in ((gl0, mt0, E0, K0), (gl1, mt1, E1, K1)):
                pool.memset(gl[:, :, n:n + 8 - k], LOW)
                pool.memset(mt[:, :, k:8], LOW)
            pool.drain().then_inc(pool_drained, 1)
            pool.wait_ge(pool_drained, 1)
            pool.affine_select(out=ident[:, :], in_=ident[:, :], compare_op=ALU.not_equal, fill=1.0, base=0,
                               pattern=[[-1, P]], channel_multiplier=1).then_inc(consts, 1)

            def split(hi, lo, src, n):
                pool.sem_inc(waited_apart, 1)
                pool.tensor_copy(hi[:, :], src).then_inc(hi_done, 1)
                pool.wait_ge(hi_done, n)
                pool.tensor_tensor(lo[:, :], src, hi[:, :].bitcast(F32), ALU.subtract).then_inc(split_ready, 1)

            def step(name, j, t):
                if name == "ctx_split":
                    pool.wait_ge(ctx_loaded, 16 * t + 16)
                    at_least(pool, full[1], use(1, "h0", E0 - 1, t - 1))
                    split(op_hi, op_lo, ctx_t[:, :], 3 * t + 1)
                elif name == "ln_stats":
                    base = POOL_STEPS * t + (0, 0, 1, 7, 8)[j]
                    var = mv[:, :, 1]
                    pool.wait_ge(var_ready, 4 * t + j)
                    pool.tensor_tensor(ve[:, :], var, eps_c[:, :], ALU.add).then_inc(pool_step, 1)
                    pool.wait_ge(pool_step, base + 1)
                    if j != 2:
                        pool.tensor_tensor(rstd[:, :], ve[:, :], minus_half[:, :], ALU.pow).then_inc(rstd_ready, 1)
                    else:
                        pool.tensor_tensor(rstd[:, :], ve[:, :], minus_half[:, :], ALU.pow).then_inc(pool_step, 1)
                        pool.wait_ge(pool_step, base + 2)
                        pool.tensor_tensor(ms[:, :], var, rstd[:, :], ALU.mult).then_inc(pool_step, 1)
                        pool.wait_ge(pool_step, base + 3)
                        pool.tensor_tensor(ms[:, :], ms[:, :], rstd[:, :], ALU.mult).then_inc(pool_step, 1)
                        pool.wait_ge(pool_step, base + 4)
                        pool.tensor_tensor(ms[:, :], ms[:, :], eps_c[:, :], ALU.add).then_inc(pool_step, 1)
                        pool.wait_ge(pool_step, base + 5)
                        pool.tensor_tensor(ms[:, :], ms[:, :], minus_half[:, :], ALU.pow).then_inc(pool_step, 1)
                        pool.wait_ge(pool_step, base + 6)
                        pool.tensor_tensor(rt[:, :], ms[:, :], rstd[:, :], ALU.mult).then_inc(rstd_ready, 1)
                    if j in (1, 3):
                        src, dst, bo = (x_in, x1, bo0_b) if j == 1 else (x1, x3, bo1_b)
                        if first(t) and j == 1:
                            pool.wait_ge(loaded["small"], 128)
                        pool.tensor_tensor(dst[:, :, :], src[:, :, :], bo[:, :].unsqueeze(1).to_broadcast([P, SUBS, D]),
                                           ALU.add).then_inc(bias_added, 1)
                    if first(t) and j == 1:
                        pool.wait_ge(loaded["w10"], 16)
                        raw = raw10.rearrange("p a (b i) -> p (a b) i", i=P)
                        pool.tensor_copy(w10_hi[:, :, :], raw).then_inc(prep_g, 1)
                        pool.wait_ge(prep_g, 1)
                        pool.tensor_tensor(w10_lo[:, :, :], raw, w10_hi[:, :, :].bitcast(F32),
                                           ALU.subtract).then_inc(prep_g, 1)
                        pool.wait_ge(prep_g, 2)
                        pool.wait_ge(prep_v, 3)
                        pool.memset(Kb[:, :, :], 0.0).then_inc(prep_g, 1)
                elif name == "ln_apply" and j == 2:
                    pool.wait_ge(z_ready, 4 * t + 2)
                    pool.tensor_tensor(x1[:, :, :], x1[:, :, :], z[:, :, :], ALU.add).then_inc(x1z_ready, 1)
                elif name == "T" and j in (2, 4):
                    wait_emptied(pool, 4, name, j, t)
                    if j == 2:
                        split(op_hi, op_lo, zT[:, :], 3 * t + 2)
                    else:
                        at_least(pool, full[6], use(6, "h1", E1 * C1 - 1, t - 1))
                        split(in1_hi, in1_lo, zT[:, :], 3 * t + 3)
                elif name in ("norm0", "norm1"):
                    h, k = (H0, j) if name == "norm0" else (H1, SUBS + j)
                    e = ex[:, j % 2, 0:SEQ * h].rearrange("p (h m) -> p h m", h=h)
                    pool.wait_ge(inv_done, SOFT * t + k + 1)
                    pool.tensor_tensor(e, e, ri[:, j % 2, 0:h].unsqueeze(2).to_broadcast([P, h, SEQ]),
                                       ALU.mult).then_inc(prob_ready, 1)

            tiles(pool, step)


_OUT = [((16, 128, 4, 128), "float32")]


def kernel(**inputs):
    import numpy as _np
    import concourse.bacc as _bacc
    from concourse import mybir as _mybir
    from concourse.bass_utils import run_bass_kernel_spmd as _run

    v = {k: _np.asarray(a) for k, a in inputs.items()}
    B, S, Dm = v["x"].shape
    T = B * S // TILE

    def heads_first(w):
        return w.T.reshape(H0, DH0, Dm).transpose(1, 0, 2).reshape(DH0, H0 * Dm)

    laid = {
        "x": v["x"].reshape(T, SUBS, P, Dm).transpose(0, 2, 1, 3),
        "ctxT": v["ctx_1024"].reshape(T, TILE, Dm).transpose(0, 2, 1),
        "wq0T": heads_first(v["L0_xattn_Wq"]),
        "wk0T": heads_first(v["L0_xattn_Wk"]),
        "wv0T": heads_first(v["L0_xattn_Wv"]),
        "wo0": v["L0_xattn_Wo"].reshape(H0, DH0, Dm).transpose(1, 0, 2).reshape(DH0, H0 * Dm),
        "bo0": v["L0_xattn_bo"].reshape(1, Dm),
        "scale0": v["L0_ffn_scale"].reshape(Dm, 1),
        "gw0T": v["L0_ffn_gate_w"].T,
        "gb0": v["L0_ffn_gate_b"].reshape(1, E0),
        "w10T": v["L0_ffn_mlp1_w"][:, ::2, :].transpose(2, 0, 1).reshape(Dm, 4, TILE),
        "b10": v["L0_ffn_mlp1_b"][:, ::2].T,
        "w20T": v["L0_ffn_mlp2_w"].transpose(2, 0, 1),
        "b20": v["L0_ffn_mlp2_b"],
        "wq1T": v["L1_xattn_Wq"].T,
        "wk1T": v["L1_xattn_Wk"].T,
        "wv1T": v["L1_xattn_Wv"].T,
        "wo1T": v["L1_xattn_Wo"].T,
        "bo1": v["L1_xattn_bo"].reshape(1, Dm),
        "gw1T": v["L1_ffn_choice"].T,
        "w11": v["L1_ffn_W1"].transpose(1, 0, 2),
        "w21": v["L1_ffn_W2"].reshape(E1 * C1, P, Dm).transpose(1, 0, 2),
    }
    nc = _bacc.Bacc("TRN2", target_bir_lowering=False, num_devices=1)
    arrays, args = {}, []
    for name, a in laid.items():
        a = _np.ascontiguousarray(a)
        arrays[f"in_{name}_dram"] = a
        args.append(nc.dram_tensor(f"in_{name}_dram", a.shape, _mybir.dt.from_np(a.dtype), kind="ExternalInput").ap())
    for i, (shape, dtype) in enumerate(_OUT):
        dt = _mybir.dt.from_np(_np.dtype(dtype))
        args.append(nc.dram_tensor(f"out_{i}_dram", shape, dt, kind="ExternalOutput").ap())
    xffn_kernel(nc, *args)
    r = _run(nc, [arrays], core_ids=[0])
    return r.results[0]["out_0_dram"].transpose(0, 2, 1, 3).reshape(B, S, Dm)
```

```python
from contextlib import ExitStack

import concourse.bass as bass
from concourse import mybir

F32 = mybir.dt.float32
F32R = mybir.dt.float32r
ALU = mybir.AluOpType
ACT = mybir.ActivationFunctionType
AX = mybir.AxisListType

P = 128
D = 128
SEQ = 64
TILE = 512
BIASED = 3
SUBS = TILE // P
ROWS = TILE // SEQ
H0, DH0 = 8, 64
H1, DH1 = 16, 8
E0, K0 = 16, 4
E1, K1, F1 = 8, 2, 512
C1 = F1 // P
EPS = 1e-5
ALPHA, LIMIT = 1.702, 7.0
LOW = -3.0e38

BEHIND = {("ln_stats", 1): "BB", ("k0", 0): "B", ("k0", 4): "BB", ("k0", 7): "B", ("S0", 0): "BB", ("S0", 1): "B",
          ("exp0", 1): "B", ("norm0", 0): "B", ("exp0", 2): "B", ("norm0", 1): "BB", ("PT0", 1): "BBBB",
          ("PT0", 2): "BBB", ("PV0", 3): "BB", ("res0", 0): "B", ("ln_stats", 2): "BBBB", ("k1", 0): "B",
          ("T", 2): "BBBB", ("route_a", 0): "B", ("h0", 0): "B", ("route_b", 0): "B", ("s0", 0): "B",
          ("s0", 1): "BBB", ("y0", 1): "B", ("acc0", 0): "B", ("rT", 0): "BB", ("s0", 6): "B", ("y0", 5): "B",
          ("s0", 7): "B", ("h0", 10): "B", ("acc0", 7): "B", ("s0", 11): "BBB", ("h0", 14): "B", ("y0", 14): "BB",
          ("ln_stats", 3): "BBBB", ("v1", 1): "BB", ("T", 3): "BB", ("q1", 0): "BB", ("exp1", 0): "BBBB",
          ("S1", 1): "B", ("exp1", 1): "BBB", ("S1", 2): "BB", ("PT1", 0): "BB", ("S1", 3): "B", ("PT1", 1): "B",
          ("PV1", 0): "B", ("norm1", 3): "B", ("PT1", 2): "BN", ("PT1", 3): "B", ("PV1", 3): "NB",
          ("oT", 0): "NBB", ("wo", 0): "BBNNNNN", ("ln_stats", 4): "BBBBBB", ("ln_apply", 4): "BBB",
          ("T", 4): "NBBBB", ("gate", 1): "B", ("route_b", 1): "BBB"}


def attention_and_first_experts():
    steps = [("ln_stats", 1), ("k0", 0), ("k0", 1), ("ln_apply", 1)]
    for j in range(2, H0):
        steps += [("k0", j)]
        if j == 4:
            steps += [("T", 1)]
    for j in range(SUBS + 3):
        if j < SUBS:
            steps += [("S0", j), ("exp0", j)]
        if 0 <= j - 1 < SUBS:
            steps += [("norm0", j - 1)]
        if 0 <= j - 2 < SUBS:
            steps += [("PT0", j - 2)]
        if 0 <= j - 3 < SUBS:
            steps += [("PV0", j - 3)]
    steps += [("res0", 0), ("ln_stats", 2), ("k1", 0), ("ln_apply", 2), ("T", 2), ("gate", 0)]
    steps += [("route_a", 0), ("h0", 0), ("route_b", 0), ("h0", 1), ("s0", 0), ("route_c", 0)]
    for e in range(2, E0 + 3):
        if e < E0:
            steps += [("h0", e)]
        if e - 1 < E0:
            steps += [("s0", e - 1)]
        if e - 2 == E0 - 2:
            steps += [("v1", 0)]
        if e - 2 < E0:
            steps += [("y0", e - 2)]
        if 0 <= e - 3 < E0:
            if e - 3 == BIASED:
                steps += [("rT", 0), ("rb", 0)]
            steps += [("acc0", e - 3)]
    steps += [("ln_stats", 3), ("ln_apply", 3), ("v1", 1), ("T", 3), ("q1", 0)]
    for j in range(SUBS + 3):
        if j < SUBS:
            steps += [("S1", j), ("exp1", j)]
        if 0 <= j - 1 < SUBS:
            steps += [("norm1", j - 1)]
        if 0 <= j - 2 < SUBS:
            steps += [("PT1", j - 2)]
        if 0 <= j - 3 < SUBS:
            steps += [("PV1", j - 3)]
    steps += [("oT", 0), ("wo", 0), ("res1", 0), ("ln_stats", 4), ("ln_apply", 4), ("T", 4), ("gate", 1),
              ("route_a", 1), ("route_b", 1), ("route_c", 1)]
    return steps


def second_experts():
    steps = []
    for j in range(E1 * C1 + 3):
        if j < E1 * C1:
            steps += [("h1", j)]
        if 0 <= j - 1 < E1 * C1:
            steps += [("s1", j - 1)]
        if 0 <= j - 3 < E1 * C1:
            steps += [("y1", j - 3)]
            if (j - 3) % C1 == C1 - 1:
                steps += [("acc1", (j - 3) // C1)]
    return steps + [("store", 0)]


def woven(a, n, b):
    left, out = {"N": list(n), "B": list(b)}, []
    for step in a:
        out.append(("A", *step))
        out += [(part, *left[part].pop(0)) for part in BEHIND.get(step, "")]
    return out + [("B", *step) for step in left["B"]]


FIRST_STEPS = [("ctx_split", 0)] + [("v0", j) for j in range(H0)]
A_STEPS = attention_and_first_experts()
B_STEPS = second_experts()
WOVEN = woven(A_STEPS, FIRST_STEPS, B_STEPS)
LEADING = [s for s in WOVEN if s[0] != "B"]


def banks_of(name, j):
    if name in ("k0", "h0"):
        return [j % 2]
    if name in ("v0", "y0"):
        return [2 + j % 2]
    if name == "v1":
        return [1 + j]
    if name in ("k1", "q1", "gate", "oT"):
        return [0]
    if name == "wo":
        return [1]
    if name in ("T", "rT", "rb"):
        return [4]
    if name == "S0":
        return [j % 2]
    if name == "PT0":
        return [2 + j % 2]
    if name == "S1":
        return [0, 1]
    if name == "PT1":
        return [2, 3]
    if name in ("PV0", "PV1"):
        return [4] if j == SUBS - 1 else []
    if name == "h1":
        return [5 + j % 2]
    if name == "y1":
        return [7] if j % C1 == C1 - 1 else []
    return []


ROUTE_STEPS, POOL_STEPS = 8, 6

USES = {b: [s for s in FIRST_STEPS + A_STEPS + B_STEPS if b in banks_of(*s)] for b in range(8)}


def use(bank, name, j, t):
    return t * len(USES[bank]) + USES[bank].index((name, j)) + 1


def xffn_kernel(nc, x, ctxT, wq0T, wk0T, wv0T, wo0, bo0, scale0, gw0T, gb0, w10T, b10, w20T, b20,
                wq1T, wk1T, wv1T, wo1T, bo1, gw1T, w11, w21, out):
    TILES = x.shape[0]
    with ExitStack() as ctx:
        def sb(name, shape, dt=F32):
            return ctx.enter_context(nc.sbuf_tensor(name, shape, dt))

        def sem(name):
            return ctx.enter_context(nc.semaphore(name))

        A_hi = sb("A_hi", [P, H0, D], F32R)
        A_lo = sb("A_lo", [P, H0, D], F32R)
        Cw = sb("Cw", [P, 2, H0 // 2, D])
        w10_hi = sb("w10_hi", [P, E0, P], F32R)
        w10_lo = sb("w10_lo", [P, E0, P], F32R)
        w20 = sb("w20", [P, E0, D])
        w11_hi = sb("w11_hi", [P, E1 * C1, P], F32R)
        w11_lo = sb("w11_lo", [P, E1 * C1, P], F32R)
        w21_sb = sb("w21_sb", [P, E1 * C1, D])
        wq1 = sb("wq1", [P, D])
        wk1 = sb("wk1", [P, D])
        wv1 = sb("wv1", [P, 2, D])
        wo1 = sb("wo1", [P, D])
        gw0 = sb("gw0", [P, E0])
        gw1 = sb("gw1", [P, E1])
        b1c = sb("b1c", [P, E0])
        b2r = sb("b2r", [E0, D])
        scale_c = sb("scale_c", [P, 1])
        bo0_b = sb("bo0_b", [P, D])
        bo1_b = sb("bo1_b", [P, D])
        gb0_b = sb("gb0_b", [P, E0])
        ident = sb("ident", [P, P])
        eps_c = sb("eps_c", [P, SUBS])
        minus_half = sb("minus_half", [P, SUBS])
        one_eps_c = sb("one_eps_c", [P, SUBS])
        eps_sq_c = sb("eps_sq_c", [P, SUBS])
        ctx_t = sb("ctx_t", [P, TILE])
        op_hi = sb("op_hi", [P, TILE], F32R)
        op_lo = sb("op_lo", [P, TILE], F32R)
        in1_hi = sb("in1_hi", [P, TILE], F32R)
        in1_lo = sb("in1_lo", [P, TILE], F32R)
        x_in = sb("x_in", [P, SUBS, D])
        x1 = sb("x1", [P, SUBS, D])
        x3 = sb("x3", [P, SUBS, D])
        acc = sb("acc", [P, SUBS, D])
        z = sb("z", [P, SUBS, D])
        tz = sb("tz", [P, SUBS, D])
        zT = sb("zT", [P, TILE])
        kp = sb("kp", [P, H0, TILE])
        vp = sb("vp", [P, ROWS, TILE])
        Kb = sb("Kb", [P, H1, TILE])
        ex = sb("ex", [P, 2, 2 * TILE])
        pt = sb("pt", [P, 2, 2 * TILE])
        th1 = sb("th1", [P, 2, TILE])
        s1 = sb("s1", [P, 4, TILE])
        ex0 = ex[:, :, :].rearrange("p a (b n) -> p (a b) n", n=TILE)
        pt0 = pt[:, :, :].rearrange("p a (b n) -> p (a b) n", n=TILE)
        g0, th0, s0 = vp[:, 0:2, :], vp[:, 2:4, :], vp[:, 4:6, :]
        V1, qT, o1 = kp[:, 0:2, :], kp[:, 2, :], kp[:, 3, :]
        oT, kT = kp[:, 4, :], vp[:, 6, :]
        rT = vp[0:E0, 7, :]
        ex1 = [ex[:, 0, :], ex[:, 1, :], kp[:, 5:7, :].rearrange("p a n -> p (a n)")]
        raw11, raw10 = Kb[:, 0:8, :], Kb[:, 8:12, :]
        st = sb("st", [P, SUBS, 6])
        mv = sb("mv", [P, SUBS, 2])
        ve = sb("ve", [P, SUBS])
        rstd = sb("rstd", [P, SUBS])
        rt = sb("rt", [P, SUBS])
        mx = sb("mx", [P, 2, H1])
        sm = sb("sm", [P, 2, H1])
        mx0 = mx[:, :, :].rearrange("p a (b n) -> p (a b) n", n=H0)
        sm0 = sm[:, :, :].rearrange("p a (b n) -> p (a b) n", n=H0)
        ri1 = sb("ri1", [P, SUBS, H1])
        ri = ri1[:, :, 0:H0]
        gl0 = sb("gl0", [P, SUBS, E0 + 8 - K0])
        gl1 = sb("gl1", [P, SUBS, E1 + 8 - K1])
        m8 = sb("m8", [P, SUBS, 8])
        mt0 = sb("mt0", [P, SUBS, 8])
        mt1 = sb("mt1", [P, SUBS, 8])
        rep = sb("rep", [P, SUBS, E0 + 8])
        gd = sb("gd", [P, SUBS, E0])
        msk = sb("msk", [P, SUBS, E0])
        gs = sb("gs", [P, SUBS])
        gr = sb("gr", [P, SUBS])
        r0 = sb("r0", [P, SUBS, E0])
        r1 = sb("r1", [P, SUBS, E1])

        ps01 = ctx.enter_context(nc.psum_tensor("ps01", [P, 2, TILE], F32))
        ps23 = ctx.enter_context(nc.psum_tensor("ps23", [P, 2, TILE], F32))
        ps4 = ctx.enter_context(nc.psum_tensor("ps4", [P, TILE], F32))
        ps56 = ctx.enter_context(nc.psum_tensor("ps56", [P, 2, TILE], F32))
        ps7 = ctx.enter_context(nc.psum_tensor("ps7", [P, TILE], F32))
        BANK = [ps01[:, 0, :], ps01[:, 1, :], ps23[:, 0, :], ps23[:, 1, :], ps4[:, :],
                ps56[:, 0, :], ps56[:, 1, :], ps7[:, :]]

        full = [sem(f"full{b}") for b in range(8)]
        free = [sem(f"free{b}") for b in range(8)]
        loaded = {n: sem(f"loaded_{n}") for n in ("qk0", "vo0", "w1s", "w10", "w11", "small", "w20", "w21")}
        x_loaded, ctx_loaded, stored = sem("x_loaded"), sem("ctx_loaded"), sem("stored")
        banded = sem("banded")
        pool_drained = sem("pool_drained")
        waited_apart = sem("waited_apart")
        consts = sem("consts")
        prep_products = sem("prep_products")
        prep_a = sem("prep_a")
        prep_v = sem("prep_v")
        prep_g = sem("prep_g")
        bn_done = sem("bn_done")
        var_ready = sem("var_ready")
        pool_step = sem("pool_step")
        rstd_ready = sem("rstd_ready")
        rt_ready = sem("rt_ready")
        z_ready = sem("z_ready")
        z2_ready = sem("z2_ready")
        ctx_hi_done = sem("ctx_hi_done")
        ctx_split_ready = sem("ctx_split_ready")
        split_ready = sem("split_ready")
        bias_added = sem("bias_added")
        max_done = sem("max_done")
        exp_done = sem("exp_done")
        sum_done = sem("sum_done")
        inv_done = sem("inv_done")
        prob_ready = sem("prob_ready")
        x1z_ready = sem("x1z_ready")
        route_step = sem("route_step")
        gexp_done = sem("gexp_done")
        route_ready = sem("route_ready")
        tanh_done = sem("tanh_done")
        th0_ready = sem("th0_ready")
        s0_ready = sem("s0_ready")
        th1_ready = sem("th1_ready")

        SOFT = 2 * SUBS

        def at_least(eng, s, value):
            if not isinstance(value, int) or value > 0:
                eng.wait_ge(s, value)

        def wait_full(eng, b, name, j, t):
            eng.wait_ge(full[b], use(b, name, j, t))

        def wait_emptied(eng, b, name, j, t):
            at_least(eng, free[b], use(b, name, j, t))

        def wait_free(eng, b, name, j, t):
            at_least(eng, free[b], use(b, name, j, t) - 1)

        def wait_apart(eng, s, value):
            eng.wait_ge(s, value)
            eng.sem_inc(waited_apart, 1)

        def first(t):
            return isinstance(t, int) and t == 0

        def one(t):
            return slice(t, t + 1) if isinstance(t, int) else bass.ds(t, 1)

        def tiles(eng, step):
            for name, j in FIRST_STEPS:
                step(name, j, 0)
            for part, name, j in LEADING:
                step(name, j, 1 if part == "N" else 0)
            for part, name, j in WOVEN:
                step(name, j, {"B": 0, "A": 1, "N": 2}[part])
            with eng.Fori(1, TILES - 2) as i:
                for part, name, j in WOVEN:
                    step(name, j, i + {"B": 0, "A": 1, "N": 2}[part])
            for part, name, j in WOVEN:
                if part != "N":
                    step(name, j, TILES - 1 if part == "A" else TILES - 2)
            for name, j in B_STEPS:
                step(name, j, TILES - 1)

        block = ctx.enter_context(nc.Block())

        @block.sync
        def _(sp):
            def load_tile(t):
                sp.dma_start(ctx_t[:, :], ctxT[one(t)].rearrange("o p n -> (o p) n")).then_inc(ctx_loaded, 16)
                sp.dma_start(x_in[:, :, :], x[one(t)].rearrange("o p s d -> (o p) s d")).then_inc(x_loaded, 16)

            sp.dma_start(ex[0:DH0, 0, :], wk0T).then_inc(loaded["qk0"], 16)
            sp.dma_start(ex[0:DH0, 1, :], wq0T).then_inc(loaded["qk0"], 16)
            sp.dma_start(pt[0:DH0, 0, :], wv0T).then_inc(loaded["vo0"], 16)
            sp.dma_start(pt[0:DH0, 1, :], wo0).then_inc(loaded["vo0"], 16)
            load_tile(0)
            for dst, src in ((gw0, gw0T), (gw1, gw1T), (b1c, b10), (b2r, b20), (scale_c, scale0)):
                sp.dma_start(dst[:, :], src).then_inc(loaded["small"], 16)
            for dst, src in ((bo0_b, bo0), (bo1_b, bo1), (gb0_b, gb0)):
                sp.dma_start(dst[:, :], src.broadcast_to([P, src.shape[1]])).then_inc(loaded["small"], 16)
            for dst, src in ((wq1, wq1T), (wk1, wk1T), (wo1, wo1T)):
                sp.dma_start(dst[:, :], src).then_inc(loaded["w1s"], 16)
            for r in range(2):
                sp.dma_start(wv1[:, r, :], wv1T).then_inc(loaded["w1s"], 16)
            sp.dma_start(raw10, w10T).then_inc(loaded["w10"], 16)
            sp.dma_start(raw11, w11).then_inc(loaded["w11"], 16)
            sp.dma_start(w20[:, :, :], w20T).then_inc(loaded["w20"], 16)
            sp.dma_start(w21_sb[:, :, :], w21).then_inc(loaded["w21"], 16)

            def step(name, j, t):
                if name == "k1":
                    wait_emptied(sp, 0, name, j, t)
                    if first(t):
                        sp.wait_ge(prep_g, 3)
                    for h in range(H1):
                        rows = slice(DH1 * h, DH1 * h + DH1)
                        sp.dma_start(Kb[rows, h, :], kT[rows, :]).then_inc(banded, 16)
                elif name == "v1" and j == 1 and not (isinstance(t, int) and t == TILES - 1):
                    wait_emptied(sp, 2, name, j, t)
                    load_tile(t + 1)
                elif name == "store":
                    wait_emptied(sp, 7, "y1", E1 * C1 - 1, t)
                    sp.dma_start(out[one(t)].rearrange("o p s d -> (o p) s d"), acc[:, :, :]).then_inc(stored, 16)

            tiles(sp, step)
            sp.wait_ge(stored, 16 * TILES)

        @block.tensor
        def _(pe):
            def mm3(dst, l_hi, l_lo, r_hi, r_lo):
                pe.matmul(dst, l_hi, r_lo, start=True, stop=False)
                pe.matmul(dst, l_lo, r_hi, start=False, stop=False)
                return pe.matmul(dst, l_hi, r_hi, start=False, stop=True)

            pe.wait_ge(loaded["qk0"], 32)
            for h in range(H0):
                cols = slice(P * h, P * h + P)
                mm = pe.matmul(BANK[h // 4][:, P * (h % 4):P * (h % 4) + P], ex[0:DH0, 0, cols], ex[0:DH0, 1, cols],
                               start=True, stop=True, skip_group_check=True)
            mm.then_inc(prep_products, 1)
            pe.wait_ge(loaded["vo0"], 32)
            for h in range(H0):
                cols = slice(P * h, P * h + P)
                mm = pe.matmul(BANK[2 + h % 2][:, P * (h // 2):P * (h // 2) + P], pt[0:DH0, 0, cols],
                               pt[0:DH0, 1, cols], start=True, stop=True, skip_group_check=True)
            mm.then_inc(prep_products, 1)
            pe.wait_ge(consts, 1)

            def step(name, j, t):
                if name == "k0":
                    b = j % 2
                    if j == 0:
                        pe.wait_ge(ctx_split_ready, t + 1)
                        if first(t):
                            pe.wait_ge(prep_v, 1)
                    wait_free(pe, b, name, j, t)
                    mm3(BANK[b], A_hi[:, j, :], A_lo[:, j, :], op_hi[:, :], op_lo[:, :]).then_inc(full[b], 1)
                elif name == "v0":
                    b = 2 + j % 2
                    if j == 0:
                        pe.wait_ge(ctx_loaded, 16 * t + 16)
                        if first(t):
                            pe.wait_ge(prep_a, 2)
                    wait_free(pe, b, name, j, t)
                    row = ctx_t[:, SEQ * j:SEQ * j + SEQ]
                    pe.matmul(BANK[b][0:SEQ, :], row, Cw[:, 0, :, :], start=True, stop=True)
                    pe.matmul(BANK[b][SEQ:P, :], row, Cw[:, 1, :, :], start=True, stop=True).then_inc(full[b], 1)
                elif name == "k1":
                    if first(t):
                        pe.wait_ge(loaded["w1s"], 80)
                    wait_free(pe, 0, name, j, t)
                    pe.matmul(BANK[0], wk1[:, :], ctx_t[:, :], start=True, stop=True).then_inc(full[0], 1)
                elif name == "T":
                    pe.wait_ge(z_ready, 4 * t + j)
                    wait_free(pe, 4, name, j, t)
                    src = tz if j == 2 else z
                    for s in range(SUBS):
                        mm = pe.transpose(BANK[4][:, P * s:P * s + P], src[:, s, :], ident[:, :])
                    mm.then_inc(full[4], 1)
                elif name == "S0":
                    b = j % 2
                    if j == 0:
                        wait_emptied(pe, 4, "T", 1, t)
                        wait_emptied(pe, 1, "k0", H0 - 1, t)
                    wait_free(pe, b, name, j, t)
                    for r in range(2):
                        tok = slice(P * j + SEQ * r, P * j + SEQ * r + SEQ)
                        mm = pe.matmul(BANK[b][SEQ * r:SEQ * r + SEQ, :], zT[:, tok], kp[:, :, tok],
                                       start=True, stop=True)
                    mm.then_inc(full[b], 1)
                elif name == "PT0":
                    b = 2 + j % 2
                    pe.wait_ge(prob_ready, SUBS * t + j + 1)
                    wait_free(pe, b, name, j, t)
                    for i in range(H0 // 2):
                        mm = pe.transpose(BANK[b][:, P * i:P * i + P], ex0[:, j, P * i:P * i + P], ident[:, :])
                    mm.then_inc(full[b], 1)
                elif name == "PV0":
                    wait_emptied(pe, 2 + j % 2, "PT0", j, t)
                    if j == 0:
                        wait_free(pe, 4, name, SUBS - 1, t)
                    for i in range(H0 // 2):
                        for r in range(2):
                            mm = pe.matmul(BANK[4][SEQ * r:SEQ * r + SEQ, P * j:P * j + P],
                                           pt0[:, j, P * i + SEQ * r:P * i + SEQ * r + SEQ],
                                           vp[:, 2 * j + r, P * i:P * i + P],
                                           start=(i == 0), stop=(i == H0 // 2 - 1), skip_group_check=True)
                    if j == SUBS - 1:
                        mm.then_inc(full[4], 1)
                elif name == "gate":
                    wait_emptied(pe, 4, "T", 4 if j else 2, t)
                    wait_free(pe, 0, name, j, t)
                    if first(t) and j == 0:
                        pe.wait_ge(loaded["small"], 128)
                    n = E1 if j else E0
                    for s in range(SUBS):
                        mm = pe.matmul(BANK[0][:, n * s:n * s + n], zT[:, P * s:P * s + P],
                                       gw1[:, :] if j else gw0[:, :], start=True, stop=True, skip_group_check=True)
                    mm.then_inc(full[0], 1)
                elif name == "rT":
                    pe.wait_ge(route_ready, 2 * t + 1)
                    wait_free(pe, 4, name, j, t)
                    for s in range(SUBS):
                        mm = pe.transpose(BANK[4][0:E0, P * s:P * s + P], r0[:, s, :], ident[:, :])
                    mm.then_inc(full[4], 1)
                elif name == "rb":
                    wait_emptied(pe, 4, "rT", 0, t)
                    for s in range(SUBS):
                        mm = pe.matmul(BANK[4][:, P * s:P * s + P], rT[:, P * s:P * s + P], b2r[:, :],
                                       start=True, stop=True, skip_group_check=True)
                    mm.then_inc(full[4], 1)
                elif name == "h0":
                    b = j % 2
                    if j == 0:
                        pe.wait_ge(split_ready, 2 * t + 1)
                        if first(t):
                            pe.wait_ge(prep_g, 2)
                    wait_free(pe, b, name, j, t)
                    mm3(BANK[b], w10_hi[:, j, :], w10_lo[:, j, :], op_hi[:, :], op_lo[:, :]).then_inc(full[b], 1)
                elif name == "y0":
                    b = 2 + j % 2
                    pe.wait_ge(s0_ready, E0 * t + j + 1)
                    wait_free(pe, b, name, j, t)
                    if first(t) and j == 0:
                        pe.wait_ge(prep_a, 3)
                    for s in range(SUBS):
                        mm = pe.matmul(BANK[b][:, P * s:P * s + P], s0[:, j % 2, P * s:P * s + P], w20[:, j, :],
                                       start=True, stop=True, skip_group_check=True)
                    mm.then_inc(full[b], 1)
                elif name == "v1":
                    wait_free(pe, 1 + j, name, j, t)
                    if first(t) and j == 0:
                        pe.wait_ge(prep_v, 4)
                    for n in range(ROWS // 2):
                        tok = slice(SEQ * (4 * j + n), SEQ * (4 * j + n) + SEQ)
                        for r in range(2):
                            mm = pe.matmul(BANK[1 + j][SEQ * r:SEQ * r + SEQ, P * n:P * n + P], ctx_t[:, tok],
                                           wv1[:, r, :], start=True, stop=True, skip_group_check=True)
                    mm.then_inc(full[1 + j], 1)
                elif name == "q1":
                    wait_emptied(pe, 4, "T", 3, t)
                    wait_free(pe, 0, name, j, t)
                    pe.matmul(BANK[0], wq1[:, :], zT[:, :], start=True, stop=True).then_inc(full[0], 1)
                elif name == "S1":
                    if j == 0:
                        wait_emptied(pe, 0, "q1", 0, t)
                        pe.wait_ge(banded, 16 * H1 * (t + 1))
                    for b in range(2):
                        wait_free(pe, b, name, j, t)
                        for r in range(2):
                            tok = slice(P * j + SEQ * r, P * j + SEQ * r + SEQ)
                            mm = pe.matmul(BANK[b][SEQ * r:SEQ * r + SEQ, :], qT[:, tok], Kb[:, 8 * b:8 * b + 8, tok],
                                           start=True, stop=True)
                        mm.then_inc(full[b], 1)
                elif name == "PT1":
                    pe.wait_ge(exp_done, SUBS * t + j + 1)
                    for b in (2, 3):
                        wait_free(pe, b, name, j, t)
                        for i in range(4):
                            col = P * (4 * (b - 2) + i)
                            mm = pe.transpose(BANK[b][:, P * i:P * i + P], ex1[j % 3][:, col:col + P], ident[:, :])
                        mm.then_inc(full[b], 1)
                elif name == "PV1":
                    wait_emptied(pe, 3, "PT1", j, t)
                    if j == 0:
                        wait_free(pe, 4, name, SUBS - 1, t)
                    for i in range(H1 // 2):
                        for r in range(2):
                            row = 2 * j + r
                            col = P * (row % 4) + 16 * i
                            mm = pe.matmul(BANK[4][SEQ * r:SEQ * r + SEQ, P * j + 16 * i:P * j + 16 * i + 16],
                                           pt[:, j % 2, P * i + SEQ * r:P * i + SEQ * r + SEQ],
                                           V1[:, row // 4, col:col + 16], start=True, stop=True,
                                           skip_group_check=True)
                    if j == SUBS - 1:
                        mm.then_inc(full[4], 1)
                elif name == "oT":
                    wait_emptied(pe, 4, "PV1", SUBS - 1, t)
                    wait_free(pe, 0, name, j, t)
                    for s in range(SUBS):
                        mm = pe.transpose(BANK[0][:, P * s:P * s + P], o1[:, P * s:P * s + P], ident[:, :])
                    mm.then_inc(full[0], 1)
                elif name == "wo":
                    wait_emptied(pe, 0, "oT", 0, t)
                    wait_free(pe, 1, name, j, t)
                    for s in range(SUBS):
                        mm = pe.matmul(BANK[1][:, P * s:P * s + P], oT[:, P * s:P * s + P], wo1[:, :],
                                       start=True, stop=True, skip_group_check=True)
                    mm.then_inc(full[1], 1)
                elif name == "h1":
                    b = 5 + j % 2
                    if j == 0:
                        pe.wait_ge(split_ready, 2 * t + 2)
                    wait_free(pe, b, name, j, t)
                    mm3(BANK[b], w11_hi[:, j, :], w11_lo[:, j, :], in1_hi[:, :], in1_lo[:, :]).then_inc(full[b], 1)
                elif name == "y1":
                    c = j % C1
                    wait_emptied(pe, 5 + j % 2, "h1", j, t)
                    if c == 0:
                        wait_free(pe, 7, name, j + C1 - 1, t)
                    if first(t) and j == 0:
                        pe.wait_ge(prep_a, 4)
                    for s in range(SUBS):
                        mm = pe.matmul(BANK[7][:, P * s:P * s + P], s1[:, j % 4, P * s:P * s + P], w21_sb[:, j, :],
                                       start=(c == 0 and s == 0), stop=(c == C1 - 1), skip_group_check=True)
                    if c == C1 - 1:
                        mm.then_inc(full[7], 1)

            tiles(pe, step)

        @block.scalar
        def _(act):
            act.wait_ge(prep_products, 1)
            act.activation(A_hi[:, :, :], ps01[:, :, :].rearrange("p a (b d) -> p (a b) d", d=D), ACT.Copy,
                           scale=DH0 ** -0.5).then_inc(prep_a, 1)
            act.wait_ge(prep_products, 2)
            act.activation(Cw[:, :, :, :], ps23[:, :, :].rearrange("p a (b d) -> p a b d", d=D),
                           ACT.Copy).then_inc(prep_a, 1)

            def copy_out(b, dst, name, j, t, **how):
                wait_full(act, b, name, j, t)
                act.activation(dst, BANK[b], ACT.Copy, **how).then_inc(free[b], 1)

            def step(name, j, t):
                if name == "ctx_split":
                    act.wait_ge(ctx_loaded, 16 * t + 16)
                    act.activation(op_hi[:, :], ctx_t[:, :], ACT.Copy).then_inc(ctx_hi_done, 1)
                elif name == "k0":
                    copy_out(j % 2, kp[:, j, :], name, j, t)
                elif name == "v0":
                    copy_out(2 + j % 2, vp[:, j, :], name, j, t)
                elif name == "k1":
                    copy_out(0, kT, name, j, t)
                    if first(t):
                        act.wait_ge(loaded["w20"], 16)
                        act.activation(w20[:, :, :], w20[:, :, :], ACT.Copy,
                                       scale=(LIMIT + 1.0) / 2).then_inc(prep_a, 1)
                        act.wait_ge(loaded["w21"], 16)
                        act.activation(w21_sb[:, :, :], w21_sb[:, :, :], ACT.Copy, scale=0.5).then_inc(prep_a, 1)
                elif name == "T":
                    if j == 1:
                        at_least(act, split_ready, 2 * t)
                    if j in (2, 4):
                        wait_full(act, 4, name, j, t)
                        how = {"scale": scale_c[:, 0:1]} if j == 2 else {}
                        act.activation(zT[:, :], BANK[4], ACT.Copy, **how)
                        act.activation((op_hi if j == 2 else in1_hi)[:, :], BANK[4], ACT.Copy,
                                       **how).then_inc(free[4], 1)
                    else:
                        copy_out(4, zT[:, :], name, j, t)
                elif name == "exp0":
                    act.wait_ge(max_done, 3 * SUBS * t + j + 1)
                    for h in range(H0):
                        cols = slice(SEQ * h, SEQ * h + SEQ)
                        ins = act.activation(ex0[:, j, cols], BANK[j % 2][:, cols], ACT.Exp,
                                             bias=mx0[:, j, h:h + 1], accum_out=sm0[:, j, h:h + 1])
                    ins.then_inc(free[j % 2], 1)
                elif name == "exp1":
                    act.wait_ge(max_done, 3 * SUBS * t + SUBS + 2 * j + 1)
                    for h in range(8):
                        cols = slice(SEQ * h, SEQ * h + SEQ)
                        ins = act.activation(ex1[j % 3][:, cols], BANK[0][:, cols], ACT.Exp,
                                             bias=mx[:, j % 2, h:h + 1])
                    ins.then_inc(free[0], 1)
                    wait_emptied(act, 1, "S1", j, t)
                    act.activation(ex1[j % 3][:, TILE:2 * TILE], ex1[j % 3][:, TILE:2 * TILE],
                                   ACT.Exp).then_inc(exp_done, 1)
                elif name == "PT0":
                    copy_out(2 + j % 2, pt0[:, j, :], name, j, t)
                elif name == "PT1":
                    for b in (2, 3):
                        copy_out(b, pt[:, j % 2, TILE * (b - 2):TILE * (b - 1)], name, j, t)
                elif name == "route_b":
                    n = E1 if j else E0
                    act.wait_ge(route_step, ROUTE_STEPS * (2 * t + j) + 3)
                    act.activation(gd[:, :, 0:n], gd[:, :, 0:n], ACT.Exp).then_inc(gexp_done, 1)
                elif name == "rT":
                    wait_full(act, 4, name, j, t)
                    act.activation(rT, BANK[4][0:E0, :], ACT.Copy).then_inc(free[4], 1)
                elif name == "h0":
                    wait_emptied(act, j % 2, name, j, t)
                    act.activation(th0[:, j % 2, :], g0[:, j % 2, :], ACT.Tanh, scale=ALPHA / 2)\
                       .then_inc(tanh_done, 1)
                    act.wait_ge(tanh_done, E0 * t + j + 1)
                    act.activation(th0[:, j % 2, :], th0[:, j % 2, :], ACT.Copy, bias=1.0).then_inc(th0_ready, 1)
                elif name == "v1":
                    copy_out(1 + j, V1[:, j, :], name, j, t)
                elif name == "q1":
                    copy_out(0, qT, name, j, t, scale=DH1 ** -0.5)
                elif name == "oT":
                    copy_out(0, oT, name, j, t)
                elif name == "h1":
                    wait_full(act, 5 + j % 2, name, j, t)
                    act.activation(th1[:, j % 2, :], BANK[5 + j % 2], ACT.Tanh, scale=0.5).then_inc(th1_ready, 1)

            tiles(act, step)

        @block.vector
        def _(dve):
            dve.wait_ge(prep_a, 1)
            dve.scalar_tensor_tensor(out=A_lo[:, :, :], in0=ps01[:, :, :].rearrange("p a (b d) -> p (a b) d", d=D),
                                     scalar=DH0 ** -0.5, in1=A_hi[:, :, :].bitcast(F32), op0=ALU.mult,
                                     op1=ALU.subtract).then_inc(prep_v, 1)

            def row_max(b, name, j, t):
                wait_full(dve, b, name, j, t)
                m = mx[:, j % 2, 8 * b:8 * b + 8] if name == "S1" else mx0[:, j, :]
                dve.tensor_reduce(m, BANK[b].rearrange("p (h m) -> p h m", h=8), AX.X, ALU.max,
                                  negate=True).then_inc(max_done, 1)

            def step(name, j, t):
                if name == "ln_stats":
                    src = x_in if j == 1 else x1 if j < 4 else x3
                    if j == 1:
                        dve.wait_ge(x_loaded, 16 * t + 16)
                    elif j == 2:
                        wait_emptied(dve, 4, "PV0", SUBS - 1, t)
                    elif j == 3:
                        wait_emptied(dve, 3, "y0", E0 - 1, t)
                    else:
                        wait_emptied(dve, 1, "wo", 0, t)
                    for s in range(SUBS):
                        ins = dve.bn_stats(st[:, s, :], src[:, s, :])
                    ins.then_inc(bn_done, 1)
                    wait_apart(dve, bn_done, 4 * t + j)
                    for s in range(SUBS):
                        ins = dve.bn_aggr(mv[:, s, :], st[:, s, :])
                    ins.then_inc(var_ready, 1)
                elif name == "ln_apply":
                    src = x_in if j == 1 else x1 if j < 4 else x3
                    if j == 2:
                        dve.wait_ge(rt_ready, t + 1)
                        for s in range(SUBS):
                            ins = dve.tensor_scalar(tz[:, s, :], src[:, s, :], mv[:, s, 0:1], rt[:, s:s + 1],
                                                    ALU.subtract, ALU.mult)
                        ins.then_inc(z_ready, 1)
                    dve.wait_ge(rstd_ready, 4 * t + j)
                    if j == 3:
                        dve.wait_ge(x1z_ready, t + 1)
                    for s in range(SUBS):
                        ins = dve.tensor_scalar(z[:, s, :], src[:, s, :], mv[:, s, 0:1], rstd[:, s:s + 1],
                                                ALU.subtract, ALU.mult)
                    ins.then_inc(z2_ready if j == 2 else z_ready, 1)
                    if first(t) and j == 1:
                        dve.wait_ge(loaded["w11"], 16)
                        raw = raw11.rearrange("p a (b f) -> p (a b) f", f=P)
                        dve.tensor_copy(w11_hi[:, :, :], raw).then_inc(prep_v, 1)
                        dve.wait_ge(prep_v, 2)
                        dve.tensor_tensor(w11_lo[:, :, :], raw, w11_hi[:, :, :].bitcast(F32),
                                          ALU.subtract).then_inc(prep_v, 1)
                        dve.wait_ge(loaded["w1s"], 80)
                        for r in range(2):
                            pairs = wv1[:, r, :].rearrange("p (i r d) -> p i r d", r=2, d=DH1)
                            ins = dve.memset(pairs[:, :, 1 - r, :], 0.0)
                        ins.then_inc(prep_v, 1)
                elif name == "exp0":
                    row_max(j % 2, "S0", j, t)
                elif name == "exp1":
                    for b in range(2):
                        row_max(b, "S1", j, t)
                    dve.wait_ge(max_done, 3 * SUBS * t + SUBS + 2 * j + 2)
                    dve.tensor_tensor(ex1[j % 3][:, TILE:2 * TILE].rearrange("p (h m) -> p h m", h=8),
                                      BANK[1].rearrange("p (h m) -> p h m", h=8),
                                      mx[:, j % 2, 8:16].unsqueeze(2).to_broadcast([P, 8, SEQ]),
                                      ALU.add).then_inc(free[1], 1)
                elif name == "norm0":
                    wait_emptied(dve, j % 2, "S0", j, t)
                    dve.reciprocal(ri[:, j, :], sm0[:, j, :]).then_inc(inv_done, 1)
                elif name == "norm1":
                    dve.wait_ge(exp_done, SUBS * t + j + 1)
                    dve.tensor_reduce(sm[:, j % 2, :], ex1[j % 3].rearrange("p (h m) -> p h m", h=H1),
                                      AX.X, ALU.add).then_inc(sum_done, 1)
                    dve.wait_ge(sum_done, SUBS * t + j + 1)
                    dve.reciprocal(ri1[:, j, :], sm[:, j % 2, :]).then_inc(inv_done, 1)
                elif name == "PV1" and j == SUBS - 1:
                    wait_full(dve, 4, name, j, t)
                    dve.wait_ge(inv_done, SOFT * t + SOFT)
                    dve.tensor_tensor(o1.rearrange("p (s d) -> p s d", d=DH1),
                                      BANK[4].rearrange("p (s d) -> p s d", d=DH1),
                                      ri1[:, :, :].rearrange("p s h -> p (s h)").unsqueeze(2)
                                      .to_broadcast([P, SUBS * H1, DH1]), ALU.mult).then_inc(free[4], 1)
                elif name == "res0":
                    wait_full(dve, 4, "PV0", SUBS - 1, t)
                    dve.wait_ge(bias_added, 2 * t + 1)
                    flat = x1[:, :, :].rearrange("p s d -> p (s d)")
                    dve.tensor_tensor(flat, BANK[4], flat, ALU.add).then_inc(free[4], 1)
                elif name == "res1":
                    wait_full(dve, 1, "wo", 0, t)
                    dve.wait_ge(bias_added, 2 * t + 2)
                    flat = x3[:, :, :].rearrange("p s d -> p (s d)")
                    dve.tensor_tensor(flat, BANK[1], flat, ALU.add).then_inc(free[1], 1)
                elif name == "rb":
                    wait_full(dve, 4, name, j, t)
                    wait_emptied(dve, 2 + (BIASED - 1) % 2, "y0", BIASED - 1, t)
                    flat = x1[:, :, :].rearrange("p s d -> p (s d)")
                    dve.tensor_tensor(flat, BANK[4], flat, ALU.add).then_inc(free[4], 1)
                elif name == "route_a":
                    n, k, gl, mt = (E1, K1, gl1, mt1) if j else (E0, K0, gl0, mt0)
                    r = ROUTE_STEPS * (2 * t + j)
                    wait_full(dve, 0, "gate", j, t)
                    got = BANK[0][:, 0:SUBS * n].rearrange("p (s e) -> p s e", s=SUBS)
                    if j:
                        dve.tensor_copy(gl[:, :, 0:n], got).then_inc(free[0], 1)
                    else:
                        dve.tensor_tensor(gl[:, :, 0:n], got, gb0_b[:, :].unsqueeze(1).to_broadcast([P, SUBS, n]),
                                          ALU.add).then_inc(free[0], 1)
                    dve.wait_ge(consts, 1)
                    wait_emptied(dve, 0, "gate", j, t)
                    for s in range(SUBS):
                        ins = dve.max(m8[:, s, :], gl[:, s, 0:n])
                    ins.then_inc(route_step, 1)
                    dve.wait_ge(route_step, r + 1)
                    dve.tensor_copy(mt[:, :, 0:k], m8[:, :, 0:k]).then_inc(route_step, 1)
                    dve.tensor_tensor(gd[:, :, 0:n], gl[:, :, 0:n], m8[:, :, 0:1].to_broadcast([P, SUBS, n]),
                                      ALU.subtract).then_inc(route_step, 1)
                elif name == "route_b":
                    n, k, gl, mt = (E1, K1, gl1, mt1) if j else (E0, K0, gl0, mt0)
                    r = ROUTE_STEPS * (2 * t + j)
                    width = n + 8 - k
                    wait_apart(dve, route_step, r + 2)
                    for s in range(SUBS):
                        ins = dve.match_replace(rep[:, s, 0:width], mt[:, s, :], gl[:, s, :], LOW)
                    ins.then_inc(route_step, 1)
                    dve.wait_ge(route_step, r + 4)
                    dve.tensor_tensor(msk[:, :, 0:n], rep[:, :, 0:n], gl[:, :, 0:n],
                                      ALU.not_equal).then_inc(route_step, 1)
                elif name == "route_c":
                    n, rr = (E1, r1) if j else (E0, r0)
                    r = ROUTE_STEPS * (2 * t + j)
                    dve.wait_ge(gexp_done, 2 * t + j + 1)
                    dve.wait_ge(route_step, r + 5)
                    dve.tensor_tensor(msk[:, :, 0:n], gd[:, :, 0:n], msk[:, :, 0:n], ALU.mult).then_inc(route_step, 1)
                    if not j:
                        dve.wait_ge(route_step, r + 6)
                    dve.tensor_reduce(gs[:, :], (gd if j else msk)[:, :, 0:n], AX.X, ALU.add).then_inc(route_step, 1)
                    dve.wait_ge(route_step, r + 7)
                    dve.reciprocal(gr[:, :], gs[:, :]).then_inc(route_step, 1)
                    dve.wait_ge(route_step, r + 8)
                    dve.tensor_tensor(rr[:, :, :], msk[:, :, 0:n], gr[:, :].unsqueeze(2).to_broadcast([P, SUBS, n]),
                                      ALU.mult).then_inc(route_ready, 1)
                elif name == "h0":
                    b = j % 2
                    if j >= 2:
                        dve.wait_ge(s0_ready, E0 * t + j - 1)
                    wait_full(dve, b, name, j, t)
                    dve.tensor_scalar(g0[:, b, :], BANK[b], b1c[:, j:j + 1], LIMIT, ALU.add,
                                      ALU.min).then_inc(free[b], 1)
                elif name == "acc0":
                    b = 2 + j % 2
                    if j == 0:
                        dve.wait_ge(x1z_ready, t + 1)
                        dve.wait_ge(route_ready, 2 * t + 1)
                    elif j == BIASED:
                        wait_emptied(dve, 4, "rb", 0, t)
                    else:
                        wait_emptied(dve, 5 - b, "y0", j - 1, t)
                    wait_full(dve, b, "y0", j, t)
                    for s in range(SUBS):
                        ins = dve.scalar_tensor_tensor(out=x1[:, s, :], in0=BANK[b][:, P * s:P * s + P],
                                                       scalar=r0[:, s, j:j + 1], in1=x1[:, s, :],
                                                       op0=ALU.mult, op1=ALU.add)
                    ins.then_inc(free[b], 1)
                elif name == "s1":
                    b = 5 + j % 2
                    dve.wait_ge(th1_ready, E1 * C1 * t + j + 1)
                    dve.scalar_tensor_tensor(out=s1[:, j % 4, :], in0=th1[:, j % 2, :], scalar=1.0, in1=BANK[b],
                                             op0=ALU.add, op1=ALU.mult).then_inc(free[b], 1)
                elif name == "acc1":
                    last = C1 * j + C1 - 1
                    if j:
                        wait_emptied(dve, 7, "y1", last - C1, t)
                    else:
                        dve.wait_ge(route_ready, 2 * t + 2)
                        at_least(dve, stored, 16 * t)
                    wait_full(dve, 7, "y1", last, t)
                    for s in range(SUBS):
                        ins = dve.scalar_tensor_tensor(out=acc[:, s, :], in0=BANK[7][:, P * s:P * s + P],
                                                       scalar=r1[:, s, j:j + 1], in1=(acc if j else x3)[:, s, :],
                                                       op0=ALU.mult, op1=ALU.add)
                    ins.then_inc(free[7], 1)

            tiles(dve, step)

        @block.gpsimd
        def _(pool):
            pool.memset(ident[:, :], 0.0)
            pool.memset(eps_c[:, :], EPS)
            pool.memset(minus_half[:, :], -0.5)
            pool.memset(one_eps_c[:, :], 1.0 + EPS)
            pool.memset(eps_sq_c[:, :], EPS * EPS)
            for gl, mt, n, k in ((gl0, mt0, E0, K0), (gl1, mt1, E1, K1)):
                pool.memset(gl[:, :, n:n + 8 - k], LOW)
                pool.memset(mt[:, :, k:8], LOW)
            pool.drain().then_inc(pool_drained, 1)
            pool.wait_ge(pool_drained, 1)
            pool.affine_select(out=ident[:, :], in_=ident[:, :], compare_op=ALU.not_equal, fill=1.0, base=0,
                               pattern=[[-1, P]], channel_multiplier=1).then_inc(consts, 1)

            def step(name, j, t):
                if name == "ctx_split":
                    pool.wait_ge(ctx_hi_done, t + 1)
                    pool.tensor_tensor(op_lo[:, :], ctx_t[:, :], op_hi[:, :].bitcast(F32),
                                       ALU.subtract).then_inc(ctx_split_ready, 1)
                elif name == "ln_stats":
                    base = POOL_STEPS * t + (0, 0, 1, 4, 5)[j]
                    var = mv[:, :, 1]
                    pool.wait_ge(var_ready, 4 * t + j)
                    if j == 2:
                        pool.tensor_tensor(rt[:, :], var, one_eps_c[:, :], ALU.mult).then_inc(pool_step, 1)
                        pool.wait_ge(pool_step, base + 1)
                        pool.tensor_tensor(rt[:, :], rt[:, :], eps_sq_c[:, :], ALU.add).then_inc(pool_step, 1)
                        pool.wait_ge(pool_step, base + 2)
                        pool.tensor_tensor(rt[:, :], rt[:, :], minus_half[:, :], ALU.pow).then_inc(rt_ready, 1)
                        base += 2
                    pool.tensor_tensor(ve[:, :], var, eps_c[:, :], ALU.add).then_inc(pool_step, 1)
                    pool.wait_ge(pool_step, base + 1)
                    pool.tensor_tensor(rstd[:, :], ve[:, :], minus_half[:, :], ALU.pow).then_inc(rstd_ready, 1)
                    if j in (1, 3):
                        src, dst, bo = (x_in, x1, bo0_b) if j == 1 else (x1, x3, bo1_b)
                        if first(t) and j == 1:
                            pool.wait_ge(loaded["small"], 128)
                        pool.tensor_tensor(dst[:, :, :], src[:, :, :], bo[:, :].unsqueeze(1).to_broadcast([P, SUBS, D]),
                                           ALU.add).then_inc(bias_added, 1)
                    if first(t) and j == 1:
                        pool.wait_ge(loaded["w10"], 16)
                        raw = raw10.rearrange("p a (b i) -> p (a b) i", i=P)
                        pool.tensor_copy(w10_hi[:, :, :], raw).then_inc(prep_g, 1)
                        pool.wait_ge(prep_g, 1)
                        pool.tensor_tensor(w10_lo[:, :, :], raw, w10_hi[:, :, :].bitcast(F32),
                                           ALU.subtract).then_inc(prep_g, 1)
                        pool.wait_ge(prep_g, 2)
                        pool.wait_ge(prep_v, 3)
                        pool.memset(Kb[:, :, :], 0.0).then_inc(prep_g, 1)
                elif name == "ln_apply" and j == 2:
                    pool.wait_ge(z2_ready, t + 1)
                    pool.tensor_tensor(x1[:, :, :], x1[:, :, :], z[:, :, :], ALU.add).then_inc(x1z_ready, 1)
                elif name == "T" and j in (2, 4):
                    hi, lo = (op_hi, op_lo) if j == 2 else (in1_hi, in1_lo)
                    wait_emptied(pool, 4, name, j, t)
                    pool.tensor_tensor(lo[:, :], zT[:, :], hi[:, :].bitcast(F32),
                                       ALU.subtract).then_inc(split_ready, 1)
                elif name == "s0":
                    if j >= 2:
                        wait_full(pool, 2 + j % 2, "y0", j - 2, t)
                    pool.wait_ge(th0_ready, E0 * t + j + 1)
                    pool.tensor_tensor(s0[:, j % 2, :], th0[:, j % 2, :], g0[:, j % 2, :],
                                       ALU.mult).then_inc(s0_ready, 1)
                elif name == "norm0":
                    e = ex0[:, j, :].rearrange("p (h m) -> p h m", h=H0)
                    pool.wait_ge(inv_done, SOFT * t + j + 1)
                    pool.tensor_tensor(e, e, ri[:, j, :].unsqueeze(2).to_broadcast([P, H0, SEQ]),
                                       ALU.mult).then_inc(prob_ready, 1)

            tiles(pool, step)


_OUT = [((16, 128, 4, 128), "float32")]


def kernel(**inputs):
    import numpy as _np
    import concourse.bacc as _bacc
    from concourse import mybir as _mybir
    from concourse.bass_utils import run_bass_kernel_spmd as _run

    v = {k: _np.asarray(a) for k, a in inputs.items()}
    B, S, Dm = v["x"].shape
    T = B * S // TILE

    def heads_first(w):
        return w.T.reshape(H0, DH0, Dm).transpose(1, 0, 2).reshape(DH0, H0 * Dm)

    laid = {
        "x": v["x"].reshape(T, SUBS, P, Dm).transpose(0, 2, 1, 3),
        "ctxT": v["ctx_1024"].reshape(T, TILE, Dm).transpose(0, 2, 1),
        "wq0T": heads_first(v["L0_xattn_Wq"]),
        "wk0T": heads_first(v["L0_xattn_Wk"]),
        "wv0T": heads_first(v["L0_xattn_Wv"]),
        "wo0": v["L0_xattn_Wo"].reshape(H0, DH0, Dm).transpose(1, 0, 2).reshape(DH0, H0 * Dm),
        "bo0": v["L0_xattn_bo"].reshape(1, Dm),
        "scale0": v["L0_ffn_scale"].reshape(Dm, 1),
        "gw0T": v["L0_ffn_gate_w"].T,
        "gb0": v["L0_ffn_gate_b"].reshape(1, E0),
        "w10T": v["L0_ffn_mlp1_w"][:, ::2, :].transpose(2, 0, 1).reshape(Dm, 4, TILE),
        "b10": v["L0_ffn_mlp1_b"][:, ::2].T,
        "w20T": v["L0_ffn_mlp2_w"].transpose(2, 0, 1),
        "b20": v["L0_ffn_mlp2_b"],
        "wq1T": v["L1_xattn_Wq"].T,
        "wk1T": v["L1_xattn_Wk"].T,
        "wv1T": v["L1_xattn_Wv"].T,
        "wo1T": v["L1_xattn_Wo"].T,
        "bo1": v["L1_xattn_bo"].reshape(1, Dm),
        "gw1T": v["L1_ffn_choice"].T,
        "w11": v["L1_ffn_W1"].transpose(1, 0, 2),
        "w21": v["L1_ffn_W2"].reshape(E1 * C1, P, Dm).transpose(1, 0, 2),
    }
    nc = _bacc.Bacc("TRN2", target_bir_lowering=False, num_devices=1)
    arrays, args = {}, []
    for name, a in laid.items():
        a = _np.ascontiguousarray(a)
        arrays[f"in_{name}_dram"] = a
        args.append(nc.dram_tensor(f"in_{name}_dram", a.shape, _mybir.dt.from_np(a.dtype), kind="ExternalInput").ap())
    for i, (shape, dtype) in enumerate(_OUT):
        dt = _mybir.dt.from_np(_np.dtype(dtype))
        args.append(nc.dram_tensor(f"out_{i}_dram", shape, dt, kind="ExternalOutput").ap())
    xffn_kernel(nc, *args)
    r = _run(nc, [arrays], core_ids=[0])
    return r.results[0]["out_0_dram"].transpose(0, 2, 1, 3).reshape(B, S, Dm)
```
